# Optimizing a Trainium2 kernel written in Bass

```python
import numpy as np
import jax
import jax.numpy as jnp

def _softmax(x, axis=-1):
    return jax.nn.softmax(x, axis=axis)

def _gelu(x):
    return jax.nn.gelu(x, approximate=True)

def _silu(x):
    return jax.nn.silu(x)

def _sigmoid(x):
    return jax.nn.sigmoid(x)

def _layernorm(x, axis=-1, eps=1e-05):
    m = jnp.mean(x, axis=axis, keepdims=True)
    v = jnp.var(x, axis=axis, keepdims=True)
    return (x - m) / jnp.sqrt(v + eps)

def _scatter_add(tgt, idx, src, axis=0):
    return tgt.at[idx].add(src)

def _segment_sum(src, seg, n):
    return jax.ops.segment_sum(src, seg, n)
kernel_name = 'mk_recurrent_d1_jaxref_r8_5b6736'

def setup_inputs(seed: int=0):
    np.random.seed(seed)
    _w = jnp.asarray

    def _L0_attn_setup():
        import jax, jax.numpy as jnp
        import numpy as np
        N_HEAD = 16
        PAGE_SIZE = 32
        ROPE_THETA = 10000.0

        def _rope_tables(T, D, dtype):
            inv = 1.0 / ROPE_THETA ** (np.arange(0, D, 2, dtype=np.float32) / D)
            ang = np.outer(np.arange(T, dtype=np.float32), inv)
            return (jnp.asarray(np.cos(ang), dtype), jnp.asarray(np.sin(ang), dtype))

        def _apply_rope(x, cos, sin):
            x1 = x[..., 0::2]
            x2 = x[..., 1::2]
            c = cos[None, :, None, :]
            s = sin[None, :, None, :]
            out = jnp.stack([x1 * c - x2 * s, x1 * s + x2 * c], axis=-1)
            return out.reshape(x.shape)
        key = jax.random.key(seed)
        ks = jax.random.split(key, 6)
        B, T, E = (2, 256, 128)
        L = E // 2
        sc = lambda fan: 1.0 / np.sqrt(fan)
        return {'x': jax.random.normal(ks[0], (B, T, E), jnp.float32), 'wq': jax.random.normal(ks[1], (E, E), jnp.float32) * sc(E), 'w_down': jax.random.normal(ks[2], (E, L), jnp.float32) * sc(E), 'wk_up': jax.random.normal(ks[3], (L, E), jnp.float32) * sc(L), 'wv_up': jax.random.normal(ks[4], (L, E), jnp.float32) * sc(L), 'wo': jax.random.normal(ks[5], (E, E), jnp.float32) * sc(E)}
    _L0_attn_in = _L0_attn_setup()

    def _L0_ffn_setup():
        import jax, jax.numpy as jnp
        import numpy as np
        B, F, D, H, E, K = (4, 256, 128, 256, 8, 2)
        key = jax.random.key(seed)
        ks = jax.random.split(key, 9)
        sc = lambda k, shape, fan_in: jax.random.normal(k, shape, jnp.float32) * fan_in ** (-0.5)
        return {'x': jax.random.normal(ks[0], (B, F, D), jnp.float32), 'rw1': sc(ks[1], (D, D), D), 'rb1': jnp.zeros((D,), jnp.float32), 'rw2': sc(ks[2], (D, E), D), 'rb2': jnp.zeros((E,), jnp.float32), 'ew1': sc(ks[3], (E, D, H), D), 'eb1': jnp.zeros((E, H), jnp.float32), 'ew2': sc(ks[4], (E, H, D), H), 'eb2': jnp.zeros((E, D), jnp.float32)}
    _L0_ffn_in = _L0_ffn_setup()
    _d = {'L0_attn_x': _L0_attn_in['x'], 'L0_attn_wq': _L0_attn_in['wq'], 'L0_attn_w_down': _L0_attn_in['w_down'], 'L0_attn_wk_up': _L0_attn_in['wk_up'], 'L0_attn_wv_up': _L0_attn_in['wv_up'], 'L0_attn_wo': _L0_attn_in['wo'], 'L0_ffn_rw1': _L0_ffn_in['rw1'], 'L0_ffn_rb1': _L0_ffn_in['rb1'], 'L0_ffn_rw2': _L0_ffn_in['rw2'], 'L0_ffn_rb2': _L0_ffn_in['rb2'], 'L0_ffn_ew1': _L0_ffn_in['ew1'], 'L0_ffn_eb1': _L0_ffn_in['eb1'], 'L0_ffn_ew2': _L0_ffn_in['ew2'], 'L0_ffn_eb2': _L0_ffn_in['eb2']}
    _x0 = _d['L0_attn_x']
    _d['L0_attn_x'] = jax.random.normal(jax.random.fold_in(jax.random.key(seed), 1), (8, 512, 128), dtype=_x0.dtype)
    del _x0
    return _d

def reference(L0_attn_x, L0_attn_wq, L0_attn_w_down, L0_attn_wk_up, L0_attn_wv_up, L0_attn_wo, L0_ffn_rw1, L0_ffn_rb1, L0_ffn_rw2, L0_ffn_rb2, L0_ffn_ew1, L0_ffn_eb1, L0_ffn_ew2, L0_ffn_eb2):

    def _L0_attn_ref(x, wq, w_down, wk_up, wv_up, wo):
        import jax, jax.numpy as jnp
        import numpy as np
        N_HEAD = 16
        PAGE_SIZE = 32
        ROPE_THETA = 10000.0

        def _rope_tables(T, D, dtype):
            inv = 1.0 / ROPE_THETA ** (np.arange(0, D, 2, dtype=np.float32) / D)
            ang = np.outer(np.arange(T, dtype=np.float32), inv)
            return (jnp.asarray(np.cos(ang), dtype), jnp.asarray(np.sin(ang), dtype))

        def _apply_rope(x, cos, sin):
            x1 = x[..., 0::2]
            x2 = x[..., 1::2]
            c = cos[None, :, None, :]
            s = sin[None, :, None, :]
            out = jnp.stack([x1 * c - x2 * s, x1 * s + x2 * c], axis=-1)
            return out.reshape(x.shape)
        B, T, E = x.shape
        H = N_HEAD
        D = E // H
        q = (x @ wq).reshape(B, T, H, D)
        lat = x @ w_down
        k = (lat @ wk_up).reshape(B, T, H, D)
        v = (lat @ wv_up).reshape(B, T, H, D)
        cos, sin = _rope_tables(T, D, x.dtype)
        q = _apply_rope(q, cos, sin)
        k = _apply_rope(k, cos, sin)
        scale = 1.0 / jnp.sqrt(jnp.asarray(D, x.dtype))
        scores = jnp.einsum('bqhd,bkhd->bhqk', q, k) * scale
        pages = jnp.arange(T) // PAGE_SIZE
        allowed = pages[None, :] <= pages[:, None]
        scores = jnp.where(allowed[None, None], scores, jnp.finfo(scores.dtype).min)
        attn = jax.nn.softmax(scores, axis=-1)
        out = jnp.einsum('bhqk,bkhd->bqhd', attn, v).reshape(B, T, E)
        return out @ wo

    def _L0_ffn_ref(x, rw1, rb1, rw2, rb2, ew1, eb1, ew2, eb2):
        import jax, jax.numpy as jnp
        import numpy as np
        B, F, D, H, E, K = (4, 256, 128, 256, 8, 2)
        b, f, d = x.shape
        t = x.reshape(b * f, d)
        logits = jax.nn.silu(t @ rw1 + rb1) @ rw2 + rb2
        vals, idx = jax.lax.top_k(logits, K)
        rows = jnp.arange(t.shape[0])[:, None]
        masked = jnp.full_like(logits, -jnp.inf).at[rows, idx].set(vals)
        w = jax.nn.softmax(masked, axis=1)
        eh = jax.nn.silu(jnp.einsum('td,edh->teh', t, ew1) + eb1[None])
        eo = jnp.einsum('teh,ehd->ted', eh, ew2) + eb2[None]
        y = t + jnp.einsum('te,ted->td', w, eo)
        return y.reshape(b, f, d)
    x = L0_attn_x
    xn = _layernorm(x, axis=-1)
    s = _L0_attn_ref(xn, L0_attn_wq, L0_attn_w_down, L0_attn_wk_up, L0_attn_wv_up, L0_attn_wo)
    g = _silu(_L0_ffn_ref(xn, L0_ffn_rw1, L0_ffn_rb1, L0_ffn_rw2, L0_ffn_rb2, L0_ffn_ew1, L0_ffn_eb1, L0_ffn_ew2, L0_ffn_eb2))
    x = x + s * g
    return x

_drawn_inputs = setup_inputs


def setup_inputs(seed=0):
    import zlib

    import numpy as np

    out = dict(_drawn_inputs(seed))
    spreads = {'L0_ffn_rb1': (0.0, 0.65),
     'L0_ffn_rb2': (0.0, 0.52),
     'L0_ffn_eb1': (0.0, 0.8),
     'L0_ffn_eb2': (0.0, 0.8)}
    factors = {}
    for name, (base, spread) in spreads.items():
        noise = np.random.default_rng([zlib.crc32(name.encode()), seed]).standard_normal(out[name].shape)
        drawn = base * np.exp(spread * noise) if base else spread * noise
        out[name] = jnp.asarray(drawn.astype(out[name].dtype))
    for name, factor in factors.items():
        out[name] = (out[name] * factor).astype(out[name].dtype)
    return out
```

```python
from contextlib import ExitStack

import numpy as np
import concourse.bass as bass
from concourse import mybir

F32 = mybir.dt.float32
F32R = mybir.dt.float32r
ALU = mybir.AluOpType
ACT = mybir.ActivationFunctionType
AX = mybir.AxisListType.X

P = 128
B, T, E = 8, 512, 128
H, D = 16, 8
L = E // 2
PAGE = 32
NE, HID = 8, 256
TT = T // P
NG = 4
GH = H // NG
HALVES = HID // P
NL1 = NE * HALVES
NMAX = NG * TT * (GH // 2)
NSTEP = NG * 3
SCALE = float(np.float32(1.0) / np.sqrt(np.float32(D)))
BIG = float(2.0 ** 100)
EPS = 1e-5
MASK0, MAX0 = 96, 96 + 3 * TT
MAX_SLOT = 8
EH_RING = 4


def stage_b():
    seq = [("router", 0)]
    m = 0
    for e in range(NE):
        for half in range(HALVES):
            seq.append(("layer1", HALVES * e + half))
            if e == 0 and half == 1:
                seq.append(("logits", 0))
            for _ in range(NMAX // NL1):
                seq.append(("max", m))
                m += 1
        if e == 1:
            seq += [("weights", 0), ("out_rows", 0)]
        if e >= 1:
            seq.append(("layer2", e - 1))
        seq += {1: [("out_rows", 1)], 2: [("out_rows", 2), ("out_rows", 3)],
                3: [("weights_t", 0), ("out_cols", 0), ("neg_max", 0)], 4: [("project", 0)],
                5: [("neg_max", 1), ("norm", 0)], 7: [("neg_max", 2)]}.get(e, [])
    seq += [("layer2", NE - 1), ("expert_bias", 0)]
    return seq


def stage_c():
    extra = {1: [("neg_max", 3), ("x_cols", 0)], 2: [("proj", 0)], 3: [("proj", 1)],
             4: [("proj", 2)], 5: [("proj", 3)], NSTEP: [("values", 0)]}
    seq = []
    for n in range(NSTEP + 1):
        if n < NSTEP:
            seq.append(("scores", n))
        if n >= 1:
            seq.append(("pv", n - 1))
        seq += extra.get(n, [])
    return seq


STAGE_B, STAGE_C = stage_b(), stage_c()
FINAL = ("out_rows", "out_cols", "project")
AHEAD = ("x_cols", "proj", "values", "norm")
MISC = ("router", "logits", "layer2", "out_rows", "out_cols", "project", "weights_t", "neg_max",
        "expert_bias", "x_cols", "proj", "values")


def misc_jobs(first):
    return [s for s in STAGE_B + STAGE_C if s[0] in MISC and not (first and s[0] in FINAL)]


PER_BATCH = len(misc_jobs(False)) // 2
PROLOGUE = [s for s in STAGE_C if s[0] in ("x_cols", "proj", "values")]
assert len(misc_jobs(False)) % 2 == 0 and len(PROLOGUE) % 2 == 0


def build(nc, x, wq, w_down, wk_up, wv_up, wo, rw1, rb1, rw2, rb2, ew1, eb1, ew2, eb2,
          cos_t, sin_t, ident_c, key_rows, query_rows, head_mask, rank_c, out):
    ctx = ExitStack()
    with ctx:
        def sb(name, shape, dt=F32):
            return ctx.enter_context(nc.sbuf_tensor(name, shape, dt))

        def sem(name):
            return ctx.enter_context(nc.semaphore(name))

        w_in = sb("w_in", [P, 5, E])
        kv_up = sb("kv_up", [L, 2 * E])
        wd_t = sb("wd_t", [L, E])
        w_att = sb("w_att", [P, 4, E])
        w_att_hi = sb("w_att_hi", [P, 4, E], F32R)
        w_att_lo = sb("w_att_lo", [P, 4, E], F32R)
        w_v = sb("w_v", [P, E])
        rw1_hi = sb("rw1_hi", [P, E], F32R)
        rw1_lo = sb("rw1_lo", [P, E], F32R)
        rw2_sb = sb("rw2_sb", [P, NE])
        rb2_bc = sb("rb2_bc", [P, NE])
        ew1_hi = sb("ew1_hi", [P, NE, HID], F32R)
        ew1_lo = sb("ew1_lo", [P, NE, HID], F32R)
        ew2_sb = sb("ew2_sb", [P, NE, HALVES, E])
        bias_rows = sb("bias_rows", [NL1 + 1, P])
        bias_cols = sb("bias_cols", [P, NL1 + 1])
        eb2_blocks = sb("eb2_blocks", [TT * NE, TT * E])
        cos_sb = sb("cos_sb", [P, T])
        sin_sb = sb("sin_sb", [P, T])
        ident = sb("ident", [P, P])
        mask_sb = sb("mask_sb", [P, T])
        hmask = sb("hmask", [P, GH])
        rank = sb("rank", [P, NE])
        half_exp = sb("half_exp", [P, TT])

        x_all = sb("x_all", [P, B, TT, E])
        xn = sb("xn", [P, TT, E])
        x_hi = sb("x_hi", [P, T], F32R)
        x_lo = sb("x_lo", [P, T], F32R)
        x_col = sb("x_col", [P, T])
        stats = sb("stats", [P, TT, 6])
        mv = sb("mv", [P, 5, TT])
        mean = sb("mean", [P, TT])
        var_eps = sb("var_eps", [P, TT])
        rstd = sb("rstd", [P, TT])

        rope_t = sb("rope_t", [P, 2, 2, T])
        roped = sb("roped", [P, 2, T])
        roped_hi = sb("roped_hi", [P, 2, T], F32R)
        roped_lo = sb("roped_lo", [P, 2, T], F32R)
        q_stack = sb("q_stack", [P, NG, T], F32R)
        k_stack = sb("k_stack", [P, NG, T])
        k_head = sb("k_head", [P, H, T], F32R)
        row_max = sb("row_max", [P, NG, TT, GH])
        neg_max = sb("neg_max", [P, NG, TT, MAX_SLOT])
        neg_rows = sb("neg_rows", [MAX_SLOT, NG, T])
        v_cols = sb("v_cols", [P, TT, H, 32])
        probs = sb("probs", [P, 2, GH, T])
        o_cols = sb("o_cols", [P, NG, T])
        inv_sum = sb("inv_sum", [P, TT, H])
        o_rows = sb("o_rows", [P, TT, E])
        o_t = sb("o_t", [P, T])
        gated = sb("gated", [P, TT, E])
        out_sb = sb("out_sb", [P, TT, E])

        r_act = sb("r_act", [P, T])
        lg = sb("lg", [P, 10, TT, NE])
        top = sb("top", [P, 8, TT])
        gate_w = sb("gate_w", [P, TT, NE])
        gate_t = sb("gate_t", [TT * NE, P])
        eh = sb("eh", [P, EH_RING, T])
        acc = sb("acc", [P, TT, E])
        y_sum = sb("y_sum", [P, TT, E])
        g_silu = sb("g_silu", [P, TT, E])

        bank = [ctx.enter_context(nc.psum_tensor(f"bank{i}", [P, T], F32)) for i in range(4, 8)]
        ring = ctx.enter_context(nc.psum_tensor("ring", [P, 4, T], F32))
        wide = bank[0:2]
        misc = bank[2:4]

        s_att_w, s_kv_w, s_const, s_table, s_rw, s_e1, s_e2 = (
            sem(n) for n in ("s_att_w", "s_kv_w", "s_const", "s_table", "s_rw", "s_e1", "s_e2"))
        s_x0, s_x = sem("s_x0"), sem("s_x")
        prep_dve, prep_pe, prep_act = sem("prep_dve"), sem("prep_pe"), sem("prep_act")
        var_ready, rstd_ready, xn_ready = sem("var_ready"), sem("rstd_ready"), sem("xn_ready")
        x_hi_ready, x_lo_ready = sem("x_hi_ready"), sem("x_lo_ready")
        rope_ready, roped_ready = sem("rope_ready"), sem("roped_ready")
        hi_ready, lo_ready = sem("hi_ready"), sem("lo_ready")
        q_in = [sem(f"q_in{g}") for g in range(NG)]
        k_in = [sem(f"k_in{g}") for g in range(NG)]
        k_head_ready = sem("k_head_ready")
        max_full, max_done = sem("max_full"), sem("max_done")
        neg_ready, neg_rows_ready = sem("neg_ready"), sem("neg_rows_ready")
        neg_in = [sem(f"neg_in{g}") for g in range(NG)]
        hidden_full, hidden_done = sem("hidden_full"), sem("hidden_done")
        experts_done = sem("experts_done")
        r_ready, gap_ready, tanh_ready = sem("r_ready"), sem("gap_ready"), sem("tanh_ready")
        w_ready, wt_ready = sem("w_ready"), sem("wt_ready")
        y_ready, g_ready = sem("y_ready"), sem("g_ready")
        st_full, exp_done, pv_done, o_done = (sem(n) for n in ("st_full", "exp_done", "pv_done", "o_done"))
        v_ready = sem("v_ready")
        rows_ready, o_t_ready, gated_ready = sem("rows_ready"), sem("o_t_ready"), sem("gated_ready")
        out_ready, stored = sem("out_ready"), sem("stored")
        misc_full = [sem("misc_full0"), sem("misc_full1")]
        misc_free = [sem("misc_free0"), sem("misc_free1")]
        dve_step, pool_step, act_step = sem("dve_step"), sem("pool_step"), sem("act_step")

        class Jobs:

            def __init__(self, jobs, base):
                self.at = {j: (i % 2, i // 2) for i, j in enumerate(jobs)}
                self.base = base

            def __call__(self, step):
                which, n = self.at[step]
                return which, self.base + n

        def jobs_of(b, first):
            if first:
                return Jobs(misc_jobs(True), len(PROLOGUE) // 2)
            return Jobs(misc_jobs(False), b * PER_BATCH)

        def wait_full(eng, jobs, step):
            which, n = jobs(step)
            eng.wait_ge(misc_full[which], n + 1)
            return misc[which], misc_free[which]

        def walk(do, b, first, last):
            jobs = jobs_of(b, first)
            for kind, n in STAGE_B + STAGE_C:
                if (kind in FINAL and first) or (kind in AHEAD and last):
                    continue
                if kind in do:
                    do[kind](b - 1 if kind in FINAL else b + 1 if kind in AHEAD else b, n, jobs)

        def prologue(do):
            jobs = Jobs(PROLOGUE, 0)
            for kind, n in [("norm", 0)] + PROLOGUE:
                if kind in do:
                    do[kind](0, n, jobs)

        def epilogue(do):
            final = [s for s in STAGE_B if s[0] in FINAL]
            done_before = [PER_BATCH * B - (len(PROLOGUE) // 2)] * 2
            jobs = Jobs(final, done_before[0])
            for kind, n in final:
                if kind in do:
                    do[kind](B - 1, n, jobs)

        def run(eng, do):
            prologue(do)
            walk(do, 0, True, False)
            with eng.Fori(1, B - 1) as b:
                walk(do, b, False, False)
            walk(do, B - 1, False, True)
            epilogue(do)

        def later(b, base):
            return not (isinstance(b, int) and b < base)

        block = ctx.enter_context(nc.Block())

        @block.sync
        def _(sp):
            tokens = x.rearrange("b (t p) e -> p b t e", p=P)
            sp.dma_start(x_all[:, 0, :, :], tokens[:, 0]).then_inc(s_x0, 16)
            sp.dma_start(ident[:], ident_c).then_inc(s_att_w, 16)
            sp.dma_start(w_in[:, 0, :], wq).then_inc(s_att_w, 16)
            sp.dma_start(w_in[:, 1, 0:L], w_down).then_inc(s_kv_w, 16)
            sp.dma_start(kv_up[:, 0:E], wk_up).then_inc(s_kv_w, 16)
            sp.dma_start(kv_up[:, E:2 * E], wv_up).then_inc(s_kv_w, 16)
            sp.dma_start(cos_sb[:], cos_t).then_inc(s_table, 16)
            sp.dma_start(sin_sb[:], sin_t).then_inc(s_table, 16)
            sp.dma_start(mask_sb[MASK0:P, :], query_rows).then_inc(s_const, 16)
            for g in range(NG):
                sp.dma_start(k_stack[MASK0:P, g, :], key_rows).then_inc(s_const, 16)
            sp.dma_start(hmask[:], head_mask).then_inc(s_const, 16)
            sp.dma_start(rank[:], rank_c.partition_broadcast(P)).then_inc(s_rw, 16)
            sp.dma_start(rb2_bc[:], rb2.partition_broadcast(P)).then_inc(s_rw, 16)
            sp.dma_start(w_in[:, 2, :], rw1).then_inc(s_rw, 16)
            sp.dma_start(w_in[:, 3, :], wo).then_inc(s_rw, 16)
            sp.dma_start(rw2_sb[:], rw2).then_inc(s_rw, 16)
            sp.dma_start(bias_rows[0:NL1, :], eb1.rearrange("e (f p) -> (e f) p", p=P)).then_inc(s_rw, 16)
            sp.dma_start(bias_rows[NL1:NL1 + 1, :], rb1.unsqueeze(0)).then_inc(s_rw, 16)
            sp.dma_start(probs[:].rearrange("p a h t -> p (a h t)")[:, 0:NE * HID].rearrange(
                "p (e h) -> p e h", e=NE), ew1.rearrange("e d h -> d e h")).then_inc(s_e1, 16)
            sp.dma_start(ew2_sb[:], ew2.rearrange("e (f p) d -> p e f d", p=P)).then_inc(s_e2, 16)
            for t in range(TT):
                sp.dma_start(x_all[:, 1:B, t, :], tokens[:, 1:B, t]).then_inc(s_x, 16)
            sp.wait_ge(prep_dve, 1)
            for t in range(TT):
                sp.dma_start(eb2_blocks[NE * t:NE * t + NE, t * E:(t + 1) * E], eb2).then_inc(s_e2, 16)

            def stack(b):
                sp.wait_ge(lo_ready, 2 * b + 2)
                sp.wait_ge(hi_ready, 2 * b + 2)
                for g in range(NG):
                    if later(b, 1):
                        sp.wait_ge(pv_done, NSTEP * (b - 1) + 3 * g + 3)
                        sp.wait_ge(k_head_ready, NG * (b - 1) + g + 1)
                    rows = slice(32 * g, 32 * g + 32)
                    for slot, part in ((0, roped_hi), (1, roped_hi), (2, roped_lo)):
                        sp.dma_start(k_stack[32 * slot:32 * slot + 32, g, :],
                                     part[rows, 1, :].bitcast(F32)).then_inc(k_in[g], 16)
                    for slot, part in ((0, roped_hi), (1, roped_lo), (2, roped_hi)):
                        sp.dma_start(q_stack[32 * slot:32 * slot + 32, g, :].bitcast(F32),
                                     part[rows, 0, :].bitcast(F32)).then_inc(q_in[g], 16)

            def maxima(b, g, jobs):
                sp.wait_ge(neg_rows_ready, NG * b + g + 1)
                sp.dma_start(q_stack[MAX0:MAX0 + MAX_SLOT, g, :].bitcast(F32),
                             neg_rows[:, g, :]).then_inc(neg_in[g], 16)

            def store(b, _, jobs):
                sp.wait_ge(out_ready, b + 1)
                sp.dma_start(out[b].rearrange("(t p) e -> p t e", p=P), out_sb[:]).then_inc(stored, 16)

            def ahead(b, n, jobs):
                if n == 3:
                    stack(b)

            stack_do = {"neg_max": maxima, "project": store, "proj": ahead}
            sp.wait_ge(prep_dve, 2)
            stack(0)
            walk(dict(stack_do), 0, True, False)
            with sp.Fori(1, B - 1) as b:
                walk(stack_do, b, False, False)
            walk(stack_do, B - 1, False, True)
            epilogue(stack_do)
            sp.wait_ge(stored, 16 * B)

        @block.tensor
        def _(pe):
            mm = nc.tensor.matmul

            pe.wait_ge(s_att_w, 32)
            pe.wait_ge(s_kv_w, 48)
            nc.tensor.transpose(wide[0][0:L, 0:E], w_in[:, 1, 0:L], ident[:]).then_inc(prep_pe, 1)
            pe.wait_ge(s_rw, 16 * 7)
            nc.tensor.transpose(wide[1][:, 0:NL1 + 1], bias_rows[:], ident[0:NL1 + 1, 0:NL1 + 1]).then_inc(prep_pe, 1)
            pe.wait_ge(prep_act, 1)
            mm(wide[0][:, 0:2 * E], wd_t[:], kv_up[:], start=True, stop=True).then_inc(prep_pe, 1)

            def take(jobs, step):
                which, n = jobs(step)
                if not isinstance(n, int) or n > 0:
                    pe.wait_ge(misc_free[which], n)
                return misc[which], misc_full[which]

            def x_cols(b, n, jobs):
                pe.wait_ge(xn_ready, b + 1)
                ps, full = take(jobs, ("x_cols", n))
                for t in range(TT):
                    last = nc.tensor.transpose(ps[:, t * P:(t + 1) * P], xn[:, t, :], ident[:])
                last.then_inc(full, 1)

            def split_product(ps, w_hi, w_lo, b):
                mm(ps, w_hi, x_hi[:], start=True, stop=False)
                mm(ps, w_lo, x_hi[:], start=False, stop=False)
                return mm(ps, w_hi, x_lo[:], start=False, stop=True)

            def proj(b, n, jobs):
                if n == 0:
                    pe.wait_ge(x_hi_ready, 2 * b + 2)
                    pe.wait_ge(x_lo_ready, b + 1)
                    if isinstance(b, int) and b == 0:
                        pe.wait_ge(prep_dve, 3)
                ps, full = take(jobs, ("proj", n))
                split_product(ps[:], w_att_hi[:, n, :], w_att_lo[:, n, :], b).then_inc(full, 1)

            def values(b, n, jobs):
                ps, full = take(jobs, ("values", n))
                for t in range(TT):
                    last = mm(ps[:, t * E:(t + 1) * E], x_col[:, t * P:(t + 1) * P], w_v[:], start=True, stop=True)
                last.then_inc(full, 1)

            def router(b, n, jobs):
                if isinstance(b, int) and b == 0:
                    pe.wait_ge(prep_dve, 4)
                ps, full = take(jobs, ("router", n))
                split_product(ps[:], rw1_hi[:], rw1_lo[:], b).then_inc(full, 1)

            def logits(b, n, jobs):
                pe.wait_ge(r_ready, b + 1)
                ps, full = take(jobs, ("logits", n))
                for t in range(TT):
                    last = mm(ps[:, t * NE:(t + 1) * NE], r_act[:, t * P:(t + 1) * P], rw2_sb[:], start=True, stop=True)
                last.then_inc(full, 1)

            def layer1(b, s, jobs):
                if isinstance(b, int) and b == 0 and s == 0:
                    pe.wait_ge(prep_dve, 6)
                if s >= 2:
                    pe.wait_ge(hidden_done, NL1 * b + s - 1)
                elif later(b, 1):
                    pe.wait_ge(o_done, NG * b - 1 + s)
                e, f = divmod(s, HALVES)
                w = slice(f * P, (f + 1) * P)
                split_product(wide[s % 2][:], ew1_hi[:, e, w], ew1_lo[:, e, w], b).then_inc(hidden_full, 1)

            def layer2(b, e, jobs):
                pe.wait_ge(hidden_done, NL1 * b + HALVES * (e + 1))
                if isinstance(b, int) and b == 0 and e == 0:
                    pe.wait_ge(s_e2, 16 * (1 + TT))
                ps, full = take(jobs, ("layer2", e))
                for t in range(TT):
                    for f in range(HALVES):
                        s = HALVES * e + f
                        last = mm(ps[:, t * E:(t + 1) * E], eh[:, s % EH_RING, t * P:(t + 1) * P],
                                  ew2_sb[:, e, f, :], start=(f == 0), stop=(f == HALVES - 1))
                last.then_inc(full, 1)

            def weights_t(b, n, jobs):
                pe.wait_ge(w_ready, b + 1)
                ps, full = take(jobs, ("weights_t", n))
                nc.tensor.transpose(ps[0:TT * NE, 0:P], gate_w[:].rearrange("p t e -> p (t e)"),
                                    ident[:]).then_inc(full, 1)

            def expert_bias(b, n, jobs):
                pe.wait_ge(wt_ready, b + 1)
                ps, full = take(jobs, ("expert_bias", n))
                mm(ps[:], gate_t[:], eb2_blocks[:], start=True, stop=True).then_inc(full, 1)

            def max_scores(b, m, jobs):
                g, i, pair = m // 8, m // 2 % 4, m % 2
                if m % 8 == 0:
                    pe.wait_ge(k_head_ready, NG * b + g + 1)
                    pe.wait_ge(q_in[g], 48 * b + 48)
                if m >= 2:
                    pe.wait_ge(max_done, NMAX * b + m - 1)
                elif later(b, 1):
                    pe.wait_ge(exp_done, 4 * NSTEP * b)
                width = max(2, i + 1) * P
                for r in range(2):
                    last = mm(ring[:, 2 * (m % 2) + r, 0:width], q_stack[0:MAX0, g, i * P:(i + 1) * P],
                              k_head[0:MAX0, GH * g + 2 * pair + r, 0:width], start=True, stop=True)
                last.then_inc(max_full, 1)

            def neg_max_t(b, g, jobs):
                pe.wait_ge(neg_ready, NG * b + g + 1)
                ps, full = take(jobs, ("neg_max", g))
                for i in range(TT):
                    last = nc.tensor.transpose(ps[0:MAX_SLOT, i * P:(i + 1) * P], neg_max[:, g, i, :], ident[:])
                last.then_inc(full, 1)

            def scores(b, n, jobs):
                g, j = divmod(n, 3)
                if j == 0:
                    pe.wait_ge(neg_in[g], 16 * b + 16)
                if n == 0:
                    pe.wait_ge(max_done, NMAX * b + NMAX)
                for r in range(GH):
                    if n > 0:
                        pe.wait_ge(exp_done, 4 * NSTEP * b + 4 * (n - 1) + r + 1)
                    h = GH * g + r
                    if j < 2:
                        mm(ring[:, r, j * P:T], k_head[:, h, j * P:(j + 1) * P], q_stack[:, g, j * P:T],
                           start=True, stop=True).then_inc(st_full, 1)
                    else:
                        mm(ring[:, r, 0:2 * P], k_head[:, h, 3 * P:T], q_stack[:, g, 2 * P:T], start=True, stop=True)
                        mm(ring[:, r, 2 * P:T], k_head[:, h, 2 * P:3 * P], q_stack[:, g, 2 * P:T],
                           start=True, stop=True).then_inc(st_full, 1)

            def pv(b, n, jobs):
                g, j = divmod(n, 3)
                if n == 0:
                    pe.wait_ge(hidden_done, NL1 * b + NL1)
                    pe.wait_ge(v_ready, b + 1)
                elif j == 0 and g >= 2:
                    pe.wait_ge(o_done, NG * b + g - 1)
                pe.wait_ge(exp_done, 4 * NSTEP * b + 4 * n + 4)
                parts = ((j, j * P, j * P),) if j < 2 else ((2, 2 * P, 2 * P), (3, P, 3 * P))
                for tile, src, dst in parts:
                    for r in range(GH):
                        last = mm(wide[g % 2][32 * r:32 * r + 32, dst:T], v_cols[:, tile, GH * g + r, :],
                                  probs[:, n % 2, r, src:src + T - dst], start=(tile == 0), stop=(tile == TT - 1),
                                  skip_group_check=True)
                last.then_inc(pv_done, 1)

            def out_rows(b, i, jobs):
                if i == 0:
                    pe.wait_ge(o_done, NG * b + NG)
                ps, full = take(jobs, ("out_rows", i))
                for g in range(NG):
                    last = nc.tensor.transpose(ps[:, g * P:(g + 1) * P], o_cols[:, g, i * P:(i + 1) * P], ident[:])
                last.then_inc(full, 1)

            def out_cols(b, n, jobs):
                pe.wait_ge(rows_ready, TT * b + TT)
                ps, full = take(jobs, ("out_cols", n))
                for t in range(TT):
                    last = nc.tensor.transpose(ps[:, t * P:(t + 1) * P], o_rows[:, t, :], ident[:])
                last.then_inc(full, 1)

            def project(b, n, jobs):
                pe.wait_ge(o_t_ready, b + 1)
                ps, full = take(jobs, ("project", n))
                for t in range(TT):
                    last = mm(ps[:, t * E:(t + 1) * E], o_t[:, t * P:(t + 1) * P], w_in[:, 3, :], start=True, stop=True)
                last.then_inc(full, 1)

            run(pe, {"x_cols": x_cols, "proj": proj, "values": values, "router": router, "logits": logits,
                     "layer1": layer1, "layer2": layer2, "weights_t": weights_t, "expert_bias": expert_bias,
                     "max": max_scores, "neg_max": neg_max_t, "scores": scores, "pv": pv,
                     "out_rows": out_rows, "out_cols": out_cols, "project": project})

        @block.scalar
        def _(act):
            copy = nc.scalar.copy

            act.wait_ge(prep_pe, 1)
            copy(wd_t[:], wide[0][0:L, 0:E]).then_inc(prep_act, 1)

            def x_cols(b, n, jobs):
                ps, _ = wait_full(act, jobs, ("x_cols", n))
                copy(x_hi[:], ps[:]).then_inc(x_hi_ready, 1)
                copy(x_col[:], ps[:]).then_inc(x_hi_ready, 1)

            def proj(b, n, jobs):
                if n % 2:
                    which = n // 2
                    act.wait_ge(roped_ready, 2 * b + which + 1)
                    if which == 0 and later(b, 1):
                        for g in range(NG):
                            act.wait_ge(q_in[g], 48 * b)
                            act.wait_ge(k_in[g], 48 * b)
                    copy(roped_hi[:, which, :], roped[:, which, :]).then_inc(hi_ready, 1)

            def values(b, n, jobs):
                ps, free = wait_full(act, jobs, ("values", n))
                if later(b, 1):
                    act.wait_ge(pv_done, NSTEP * b)
                else:
                    act.wait_ge(prep_dve, 2)
                copy(v_cols[:, :, :, 0:D], ps[:].rearrange("p (t h d) -> p t h d", t=TT, h=H)).then_inc(v_ready, 1)
                act.wait_ge(v_ready, b + 1)
                act.sem_inc(free, 1)

            def router(b, n, jobs):
                if isinstance(b, int) and b == 0:
                    act.wait_ge(prep_dve, 6)
                ps, free = wait_full(act, jobs, ("router", n))
                nc.scalar.activation(r_act[:], ps[:], ACT.Silu, bias=bias_cols[:, NL1:NL1 + 1]).then_inc(r_ready, 1)
                act.wait_ge(r_ready, b + 1)
                act.sem_inc(free, 1)

            def layer1(b, s, jobs):
                act.wait_ge(hidden_full, NL1 * b + s + 1)
                if s >= EH_RING:
                    which, n = jobs(("layer2", (s - EH_RING) // HALVES))
                    act.wait_ge(misc_full[which], n + 1)
                nc.scalar.activation(eh[:, s % EH_RING, :], wide[s % 2][:], ACT.Silu,
                                     bias=bias_cols[:, s:s + 1]).then_inc(hidden_done, 1)

            def weights(b, n, jobs):
                act.wait_ge(gap_ready, b + 1)
                nc.scalar.activation(top[:, 5, :], top[:, 4, :], ACT.Tanh, scale=0.5).then_inc(tanh_ready, 1)

            def weights_t(b, n, jobs):
                ps, free = wait_full(act, jobs, ("weights_t", n))
                copy(gate_t[:], ps[0:TT * NE, 0:P]).then_inc(wt_ready, 1)
                act.wait_ge(wt_ready, b + 1)
                act.sem_inc(free, 1)

            def neg_max_t(b, g, jobs):
                ps, free = wait_full(act, jobs, ("neg_max", g))
                if later(b, 1):
                    act.wait_ge(neg_in[g], 16 * b)
                copy(neg_rows[:, g, :], ps[0:MAX_SLOT, :]).then_inc(neg_rows_ready, 1)
                act.wait_ge(neg_rows_ready, NG * b + g + 1)
                act.sem_inc(free, 1)

            def expert_bias(b, n, jobs):
                act.wait_ge(y_ready, b + 1)
                if later(b, 1):
                    act.wait_ge(gated_ready, b)
                nc.scalar.activation(g_silu[:], y_sum[:], ACT.Silu).then_inc(g_ready, 1)

            def scores(b, n, jobs):
                lo = (0, P, P)[n % 3]
                if n >= 2 or later(b, 1):
                    act.wait_ge(pv_done, NSTEP * b + n - 1)
                for r in range(GH):
                    act.wait_ge(st_full, 4 * NSTEP * b + 4 * n + r + 1)
                    nc.scalar.activation(probs[:, n % 2, r, lo:T], ring[:, r, lo:T], ACT.Exp,
                                         scale=SCALE).then_inc(exp_done, 1)

            def pv(b, n, jobs):
                g, j = divmod(n, 3)
                if j == 2:
                    act.wait_ge(pv_done, NSTEP * b + n + 1)
                    copy(o_cols[:, g, :], wide[g % 2][:]).then_inc(o_done, 1)

            def out_cols(b, n, jobs):
                ps, free = wait_full(act, jobs, ("out_cols", n))
                copy(o_t[:], ps[:]).then_inc(o_t_ready, 1)
                act.wait_ge(o_t_ready, b + 1)
                act.sem_inc(free, 1)

            run(act, {"x_cols": x_cols, "proj": proj, "values": values, "router": router, "layer1": layer1,
                      "weights": weights, "weights_t": weights_t, "neg_max": neg_max_t, "expert_bias": expert_bias,
                      "scores": scores, "pv": pv, "out_cols": out_cols})

        @block.vector
        def _(dve):
            V = nc.vector
            tt, ts, stt = V.tensor_tensor, V.tensor_scalar, V.scalar_tensor_tensor
            steps = [0, 0]

            def link(ins):
                ins.then_inc(dve_step, 1)
                steps[0] += 1
                dve.wait_ge(dve_step, steps[1] + steps[0])

            V.memset(eb2_blocks[:], 0.0).then_inc(prep_dve, 1)
            V.memset(half_exp[:], -0.5)
            V.memset(v_cols[:], 0.0).then_inc(dve_step, 1)
            dve.wait_ge(dve_step, 1)
            dve.wait_ge(s_const, 16 * (2 + NG))
            for g in range(NG):
                V.tensor_copy(q_stack[MASK0:P, g, :], mask_sb[MASK0:P, :])
            V.memset(v_cols[:, :, :, D:D + 1], 1.0).then_inc(prep_dve, 1)
            dve.wait_ge(prep_dve, 2)
            dve.wait_ge(s_att_w, 32)
            V.tensor_copy(w_att[:, 0, :], w_in[:, 0, :])
            dve.wait_ge(prep_pe, 3)
            V.tensor_copy(w_v[:], wide[0][:, E:2 * E])
            V.tensor_copy(w_att[:, 2, :], wide[0][:, 0:E]).then_inc(dve_step, 1)
            dve.wait_ge(dve_step, 2)
            for w in (0, 2):
                pairs = w_att[:, w, :].rearrange("p (i two) -> p i two", two=2)
                turned = w_att[:, w + 1, :].rearrange("p (i two) -> p i two", two=2)
                ts(turned[:, :, 0], pairs[:, :, 1], -1.0, None, ALU.mult)
                V.tensor_copy(turned[:, :, 1], pairs[:, :, 0]).then_inc(dve_step, 1)
            dve.wait_ge(dve_step, 4)
            V.tensor_copy(w_att_hi[:], w_att[:]).then_inc(dve_step, 1)
            dve.wait_ge(dve_step, 5)
            tt(w_att_lo[:], w_att[:], w_att_hi[:].bitcast(F32), ALU.subtract).then_inc(prep_dve, 1)

            def norm(b, n, jobs):
                if later(b, 1):
                    dve.wait_ge(s_x, 16 * TT)
                else:
                    dve.wait_ge(s_x0, 16)
                for t in range(TT):
                    ins = V.bn_stats(stats[:, t, :], x_all[:, b, t, :])
                link(ins)
                even, odd = stats[:, :, 0:3], stats[:, :, 3:6]
                tt(mv[:, 0, :], even[:, :, 1], odd[:, :, 1], ALU.add)
                tt(mv[:, 1, :], even[:, :, 1], odd[:, :, 1], ALU.subtract)
                link(tt(mv[:, 2, :], even[:, :, 2], odd[:, :, 2], ALU.add))
                ts(mean[:], mv[:, 0, :], 0.5, None, ALU.mult)
                ts(mv[:, 3, :], mv[:, 2, :], 1.0 / E, EPS, ALU.mult, ALU.add)
                link(tt(mv[:, 4, :], mv[:, 1, :], mv[:, 1, :], ALU.mult))
                stt(out=var_eps[:], in0=mv[:, 4, :], scalar=0.25, in1=mv[:, 3, :], op0=ALU.mult,
                    op1=ALU.add).then_inc(var_ready, 1)
                dve.wait_ge(rstd_ready, b + 1)
                for t in range(TT):
                    ins = ts(xn[:, t, :], x_all[:, b, t, :], mean[:, t:t + 1], rstd[:, t:t + 1],
                             ALU.subtract, ALU.mult)
                ins.then_inc(xn_ready, 1)

            def x_cols(b, n, jobs):
                ps, free = wait_full(dve, jobs, ("x_cols", n))
                dve.wait_ge(x_hi_ready, 2 * b + 2)
                tt(x_lo[:], ps[:], x_hi[:].bitcast(F32), ALU.subtract).then_inc(x_lo_ready, 1)
                dve.wait_ge(x_lo_ready, b + 1)
                dve.sem_inc(free, 1)

            def proj(b, n, jobs):
                ps, free = wait_full(dve, jobs, ("proj", n))
                if isinstance(b, int) and b == 0 and n == 0:
                    dve.wait_ge(s_table, 32)
                which, term = divmod(n, 2)
                if term == 0 and later(b, 1):
                    dve.wait_ge(roped_ready, 2 * b - 1 + which)
                tt(rope_t[:, which, term, :], ps[:], (cos_sb, sin_sb)[term][:], ALU.mult).then_inc(rope_ready, 1)
                dve.wait_ge(rope_ready, 4 * b + n + 1)
                dve.sem_inc(free, 1)

            def logits(b, n, jobs):
                ps, free = wait_full(dve, jobs, ("logits", n))

                def wide4(ap):
                    return ap.unsqueeze(2).to_broadcast([P, TT, NE])

                rank4 = rank[:].unsqueeze(1).to_broadcast([P, TT, NE])
                link(tt(lg[:, 0], ps[:, 0:TT * NE].rearrange("p (t e) -> p t e", e=NE),
                        rb2_bc[:].unsqueeze(1).to_broadcast([P, TT, NE]), ALU.add))
                dve.sem_inc(free, 1)
                for k in range(2):
                    a = lg[:, 5 * k]
                    eq, key, one = lg[:, 5 * k + 1], lg[:, 5 * k + 2], lg[:, 5 * k + 3]
                    link(V.tensor_reduce(top[:, k, :], a, AX, ALU.max))
                    link(tt(eq, a, wide4(top[:, k, :]), ALU.is_equal))
                    link(tt(key, eq, rank4, ALU.mult))
                    link(V.tensor_reduce(top[:, 2 + k, :], key, AX, ALU.max))
                    link(tt(one, key, wide4(top[:, 2 + k, :]), ALU.is_equal))
                    if k == 0:
                        link(stt(out=lg[:, 5], in0=one, scalar=-3.0e38, in1=a, op0=ALU.mult, op1=ALU.add))
                tt(top[:, 4, :], top[:, 1, :], top[:, 0, :], ALU.subtract).then_inc(gap_ready, 1)

            def weights(b, n, jobs):
                dve.wait_ge(tanh_ready, b + 1)
                ts(top[:, 6, :], top[:, 5, :], -0.5, 0.5, ALU.mult, ALU.add)
                link(ts(top[:, 7, :], top[:, 5, :], 0.5, 0.5, ALU.mult, ALU.add))
                tt(lg[:, 4], lg[:, 3], top[:, 6, :].unsqueeze(2).to_broadcast([P, TT, NE]), ALU.mult)
                link(tt(lg[:, 9], lg[:, 8], top[:, 7, :].unsqueeze(2).to_broadcast([P, TT, NE]), ALU.mult))
                tt(gate_w[:], lg[:, 4], lg[:, 9], ALU.add).then_inc(w_ready, 1)

            def max_scores(b, m, jobs):
                g, i, pair = m // 8, m // 2 % 4, m % 2
                dve.wait_ge(max_full, NMAX * b + m + 1)
                V.tensor_reduce(row_max[:, g, i, 2 * pair:2 * pair + 2],
                                ring[:, 2 * (m % 2):2 * (m % 2) + 2, 0:(i + 1) * P], AX, ALU.max).then_inc(max_done, 1)
                if m % 8 == 7:
                    dve.wait_ge(max_done, NMAX * b + m + 1)
                    link(ts(neg_max[:, g, :, 0:GH].bitcast(F32R), row_max[:, g], -1.0, None, ALU.mult))
                    stt(out=neg_max[:, g, :, GH:2 * GH].bitcast(F32R), in0=row_max[:, g], scalar=-1.0,
                        in1=neg_max[:, g, :, 0:GH], op0=ALU.mult, op1=ALU.subtract).then_inc(neg_ready, 1)

            def layer2(b, e, jobs):
                ps, free = wait_full(dve, jobs, ("layer2", e))
                if e == 0:
                    dve.wait_ge(w_ready, b + 1)
                for t in range(TT):
                    ins = stt(out=acc[:, t, :], in0=ps[:, t * E:(t + 1) * E], scalar=gate_w[:, t, e:e + 1],
                              in1=(xn if e == 0 else acc)[:, t, :], op0=ALU.mult, op1=ALU.add)
                link(ins)
                dve.sem_inc(free, 1)

            def expert_bias(b, n, jobs):
                ps, free = wait_full(dve, jobs, ("expert_bias", n))
                tt(y_sum[:].rearrange("p t e -> p (t e)"), acc[:].rearrange("p t e -> p (t e)"), ps[:],
                   ALU.add).then_inc(y_ready, 1)
                dve.wait_ge(y_ready, b + 1)
                dve.sem_inc(free, 1)

            def out_rows(b, i, jobs):
                ps, free = wait_full(dve, jobs, ("out_rows", i))
                cols = ps[:].rearrange("p (h c) -> p h c", h=H)
                link(V.reciprocal(inv_sum[:, i, :], cols[:, :, D]))
                tt(o_rows[:, i, :].rearrange("p (h d) -> p h d", h=H), cols[:, :, 0:D],
                   inv_sum[:, i, :].unsqueeze(2).to_broadcast([P, H, D]), ALU.mult).then_inc(rows_ready, 1)
                dve.wait_ge(rows_ready, TT * b + i + 1)
                dve.sem_inc(free, 1)

            def project(b, n, jobs):
                ps, free = wait_full(dve, jobs, ("project", n))
                dve.wait_ge(g_ready, b + 1)
                if later(b, 1):
                    dve.wait_ge(out_ready, b)
                tt(gated[:].rearrange("p t e -> p (t e)"), ps[:], g_silu[:].rearrange("p t e -> p (t e)"),
                   ALU.mult).then_inc(gated_ready, 1)
                dve.wait_ge(gated_ready, b + 1)
                dve.sem_inc(free, 1)

            do = {"norm": norm, "x_cols": x_cols, "proj": proj, "logits": logits, "weights": weights,
                  "max": max_scores, "layer2": layer2, "expert_bias": expert_bias,
                  "out_rows": out_rows, "project": project}

            steps[0], steps[1] = 0, 5
            prologue(do)
            dve.wait_ge(s_rw, 16 * 7)
            link(V.tensor_copy(rw1_hi[:], w_in[:, 2, :]))
            tt(rw1_lo[:], w_in[:, 2, :], rw1_hi[:].bitcast(F32), ALU.subtract).then_inc(prep_dve, 1)
            e1_in = probs[:].rearrange("p a h t -> p (a h t)")[:, 0:NE * HID].rearrange("p (e h) -> p e h", e=NE)
            dve.wait_ge(s_e1, 16)
            link(V.tensor_copy(ew1_hi[:], e1_in))
            dve.wait_ge(prep_dve, 4)
            tt(ew1_lo[:], e1_in, ew1_hi[:].bitcast(F32), ALU.subtract).then_inc(prep_dve, 1)
            dve.wait_ge(prep_dve, 5)
            V.tensor_copy(bias_cols[:], wide[1][:, 0:NL1 + 1]).then_inc(prep_dve, 1)
            walk(do, 0, True, False)
            before = steps[0] + steps[1]
            steps[0] = 0
            with dve.Fori(1, B - 1) as b:
                steps[1] = before + (b - 1) * PER_LINKS
                walk(do, b, False, False)
                assert steps[0] == PER_LINKS, steps
            steps[1] = before + (B - 2) * PER_LINKS
            steps[0] = 0
            walk(do, B - 1, False, True)
            epilogue(do)

        @block.gpsimd
        def _(pool):
            G = nc.gpsimd

            def norm(b, n, jobs):
                pool.wait_ge(var_ready, b + 1)
                if isinstance(b, int) and b == 0:
                    pool.wait_ge(prep_dve, 2)
                if later(b, 1):
                    pool.wait_ge(xn_ready, b)
                G.tensor_tensor(rstd[:], var_eps[:], half_exp[:], ALU.pow).then_inc(rstd_ready, 1)

            def proj(b, n, jobs):
                if n % 2 == 0:
                    return
                which = n // 2
                pool.wait_ge(rope_ready, 4 * b + 2 * which + 2)
                if later(b, 1):
                    pool.wait_ge(lo_ready, 2 * b)
                G.tensor_tensor(roped[:, which, :], rope_t[:, which, 0, :], rope_t[:, which, 1, :],
                                ALU.add).then_inc(roped_ready, 1)
                pool.wait_ge(hi_ready, 2 * b + which + 1)
                G.tensor_tensor(roped_lo[:, which, :], roped[:, which, :], roped_hi[:, which, :].bitcast(F32),
                                ALU.subtract).then_inc(lo_ready, 1)
                if n == 3:
                    key_heads(b)

            def key_heads(b):
                for g in range(NG):
                    if isinstance(b, int) and b == 0 and g == 0:
                        pool.wait_ge(s_const, 16 * (2 + NG))
                    pool.wait_ge(k_in[g], 48 * b + 48)
                    if later(b, 1):
                        pool.wait_ge(pv_done, NSTEP * (b - 1) + 3 * g + 3)
                    G.tensor_tensor(k_head[:, GH * g:GH * g + GH, :],
                                    k_stack[:, g, :].unsqueeze(1).to_broadcast([P, GH, T]),
                                    hmask[:].unsqueeze(2).to_broadcast([P, GH, T]), ALU.mult).then_inc(k_head_ready, 1)

            def project(b, n, jobs):
                pool.wait_ge(gated_ready, b + 1)
                if later(b, 1):
                    pool.wait_ge(stored, 16 * b)
                G.tensor_tensor(out_sb[:], gated[:], x_all[:, b, :, :], ALU.add).then_inc(out_ready, 1)

            run(pool, {"norm": norm, "proj": proj, "project": project})


PER_LINKS = sum({"logits": 12, "weights": 2, "layer2": 1, "out_rows": 1, "norm": 3}.get(s[0], 0)
                + (s[0] == "max" and s[1] % 8 == 7) for s in STAGE_B + STAGE_C)


_INS = ["L0_attn_x", "L0_attn_wq", "L0_attn_w_down", "L0_attn_wk_up", "L0_attn_wv_up", "L0_attn_wo",
        "L0_ffn_rw1", "L0_ffn_rb1", "L0_ffn_rw2", "L0_ffn_rb2", "L0_ffn_ew1", "L0_ffn_eb1", "L0_ffn_ew2",
        "L0_ffn_eb2"]


def shape_constants():
    inv = 1.0 / 10000.0 ** (np.arange(0, D, 2, dtype=np.float32) / D)
    ang = np.outer(np.arange(T, dtype=np.float32), inv)
    spread = lambda a: np.ascontiguousarray(np.tile(np.repeat(a.T.astype(np.float32), 2, axis=0), (H, 1)))
    t = np.arange(T)
    tile, page = t // P, t % P // PAGE
    key_rows = np.zeros((P - MASK0, T), np.float32)
    query_rows = np.zeros((P - MASK0, T), np.float32)
    for j in range(TT):
        for a in range(3):
            key_rows[3 * j + a] = (tile == j) & (page > a)
            query_rows[3 * j + a] = np.where((tile == j) & (page == a), -BIG, 0.0)
    key_rows[MAX0 - MASK0:MAX0 - MASK0 + MAX_SLOT] = 1.0
    row = np.arange(P)
    head_mask = np.zeros((P, GH), np.float32)
    for r in range(GH):
        head_mask[:, r] = ((row < MASK0) & (row % 32 // D == r)) | ((row >= MASK0) & (row < MAX0)) | (
            (row >= MAX0) & (row < MAX0 + MAX_SLOT) & ((row - MAX0) % GH == r))
    return {"cos_t": spread(np.cos(ang)), "sin_t": spread(np.sin(ang)), "ident_c": np.eye(P, dtype=np.float32),
            "key_rows": key_rows, "query_rows": query_rows, "head_mask": head_mask,
            "rank_c": np.arange(NE, 0, -1).astype(np.float32)}


def kernel(**inputs):
    import concourse.bacc as bacc
    from concourse.bass_utils import run_bass_kernel_spmd

    nc = bacc.Bacc("TRN2", target_bir_lowering=False, num_devices=1)
    arrays, args = {}, []
    for name, a in [(n, np.ascontiguousarray(inputs[n])) for n in _INS] + list(shape_constants().items()):
        arrays[f"in_{name}"] = a
        args.append(nc.dram_tensor(f"in_{name}", a.shape, mybir.dt.from_np(a.dtype), kind="ExternalInput").ap())
    args.append(nc.dram_tensor("out_0", (B, T, E), F32, kind="ExternalOutput").ap())
    build(nc, *args)
    return run_bass_kernel_spmd(nc, [arrays], core_ids=[0]).results[0]["out_0"]
```

```python
from contextlib import ExitStack

import numpy as np
import concourse.bass as bass
from concourse import mybir

F32 = mybir.dt.float32
F32R = mybir.dt.float32r
ALU = mybir.AluOpType
ACT = mybir.ActivationFunctionType
AX = mybir.AxisListType.X

P = 128
B, T, E = 8, 512, 128
H, D = 16, 8
L = E // 2
PAGE = 32
NE, HID = 8, 256
TT = T // P
NG = 4
GH = H // NG
HALVES = HID // P
NL1 = NE * HALVES
NPAIR = TT * (GH // 2)
NMAX = (NG - 1) * NPAIR
NMAX0 = TT * GH
NSTEP = NG * 3
NEXP = GH // 2
SCALE = float(np.float32(1.0) / np.sqrt(np.float32(D)))
BIG = float(2.0 ** 100)
EPS = 1e-5
MASK0, MAX0 = 96, 96 + 3 * TT
NTOP = 11
MAX_SLOT = 8
EH_RING = 4


def stage_b():
    maxima, top = iter(range(NMAX)), iter(range(NTOP))
    extra = {0: [("logits", 0)], 2: [("out_rows", 0), ("out_rows", 1)], 3: [("weights", 0), ("neg_max", 0)],
             4: [("out_rows", 2)], 5: [("weights_t", 0), ("out_rows", 3)], 6: [("negate", 1), ("stats", 0)],
             7: [("out_cols", 0), ("neg_max", 1)], 9: [("project", 0), ("norm", 0)], 11: [("negate", 2)],
             13: [("neg_max", 2)]}
    seq = [("router", 0)]
    for s in range(NL1):
        seq.append(("layer1", s))
        if s == NL1 - 1:
            seq.append(("x_cols", 0))
        for _ in range(1 + s % 2):
            seq.append(("max", next(maxima)))
            if s >= 1:
                seq += [("top", n) for _, n in zip(range(3), top)]
        seq += extra.get(s, [])
        if s == 0:
            seq.append(("heads", 3))
        if s % HALVES == 1 and s > HALVES:
            seq.append(("layer2", s // HALVES - 1))
    assert not list(maxima) and not list(top)
    return seq + [("negate", 3), ("layer2", NE - 1), ("proj", 0), ("expert_bias", 0), ("proj", 1),
                  ("neg_max", 3), ("proj", 2), ("proj", 3)]


def stage_c():
    extra = {0: [("split", 0), ("split", 1), ("stack", 0)], 4: [("stack", 1)],
             5: [("heads", 0)], 7: [("stack", 2)], 8: [("heads", 1)], 10: [("stack", 3)],
             11: [("heads", 2)], NSTEP: [("values", 0), ("negate", 0)]}
    for n in range(NMAX0):
        extra.setdefault(6 + n * 6 // NMAX0, []).append(("max0", n))
    seq = []
    for n in range(NSTEP + 1):
        if n < NSTEP:
            seq.append(("scores", n))
        if n >= 1:
            seq.append(("pv", n - 1))
        seq += extra.get(n, [])
    return seq


STAGE_B, STAGE_C = stage_b(), stage_c()
FINAL = ("out_rows", "out_cols", "project")
AHEAD = [s for s in STAGE_B if s[0] in ("stats", "norm", "x_cols", "proj")] + [
    s for s in STAGE_C if s[0] in ("split", "stack", "values", "heads", "max0", "negate")]
MISC = ("router", "logits", "layer2", "out_rows", "out_cols", "project", "weights_t", "neg_max",
        "expert_bias", "x_cols", "proj", "values", "max0")


def steps_of(first=False, last=False):
    return [s for s in STAGE_B + STAGE_C
            if not (first and s[0] in FINAL) and not (last and s in AHEAD)]


def misc_jobs(steps):
    jobs = [s for s in steps if s[0] in MISC]
    assert len(jobs) % 2 == 0
    return jobs


JOBS = {name: misc_jobs(steps) for name, steps in (
    ("prologue", AHEAD), ("first", steps_of(first=True)), ("middle", steps_of()),
    ("last", steps_of(last=True)), ("epilogue", [s for s in STAGE_B if s[0] in FINAL]))}
PER_BATCH = len(JOBS["middle"])
BEFORE = {"first": "prologue", "middle": "middle", "last": "middle", "epilogue": "last"}
assert JOBS["first"][-2:] == JOBS["middle"][-2:]


def build(nc, x, wq, w_down, wk_up, wv_up, wo, rw1, rb1, rw2, rb2, ew1, eb1, ew2, eb2,
          cos_t, sin_t, ident_c, key_rows, query_rows, head_mask, rank_c, out):
    ctx = ExitStack()
    with ctx:
        def sb(name, shape, dt=F32):
            return ctx.enter_context(nc.sbuf_tensor(name, shape, dt))

        def sem(name):
            return ctx.enter_context(nc.semaphore(name))

        w_in = sb("w_in", [P, 5, E])
        kv_up = sb("kv_up", [L, 2 * E])
        wd_t = sb("wd_t", [L, E])
        w_att = sb("w_att", [P, 4, E])
        w_att_hi = sb("w_att_hi", [P, 4, E], F32R)
        w_att_lo = sb("w_att_lo", [P, 4, E], F32R)
        w_v = sb("w_v", [P, E])
        rw1_hi = sb("rw1_hi", [P, E], F32R)
        rw1_lo = sb("rw1_lo", [P, E], F32R)
        rw2_sb = sb("rw2_sb", [P, NE])
        rb2_bc = sb("rb2_bc", [P, NE])
        ew1_hi = sb("ew1_hi", [P, NE, HID], F32R)
        ew1_lo = sb("ew1_lo", [P, NE, HID], F32R)
        ew2_sb = sb("ew2_sb", [P, NE, HALVES, E])
        bias_rows = sb("bias_rows", [NL1 + 1, P])
        bias_cols = sb("bias_cols", [P, NL1 + 1])
        eb2_blocks = sb("eb2_blocks", [TT * NE, TT * E])
        cos_sb = sb("cos_sb", [P, T])
        sin_sb = sb("sin_sb", [P, T])
        ident = sb("ident", [P, P])
        mask_sb = sb("mask_sb", [P, T])
        hmask = sb("hmask", [P, GH])
        rank = sb("rank", [P, NE])
        half_exp = sb("half_exp", [P, TT])

        x_all = sb("x_all", [P, B, TT, E])
        xn = sb("xn", [P, TT, E])
        x_hi = sb("x_hi", [P, T], F32R)
        x_lo = sb("x_lo", [P, T], F32R)
        x_col = sb("x_col", [P, T])
        stats = sb("stats", [P, TT, 6])
        mv = sb("mv", [P, 5, TT])
        mean = sb("mean", [P, TT])
        var_eps = sb("var_eps", [P, TT])
        rstd = sb("rstd", [P, TT])

        rope_t = sb("rope_t", [P, 2, 2, T])
        roped = sb("roped", [P, 2, T])
        roped_hi = sb("roped_hi", [P, 2, T], F32R)
        roped_lo = sb("roped_lo", [P, 2, T], F32R)
        q_stack = sb("q_stack", [P, NG, T], F32R)
        k_stack = sb("k_stack", [P, NG, T])
        k_head = sb("k_head", [P, H, T], F32R)
        row_max = sb("row_max", [P, NG, TT, GH])
        neg_max = sb("neg_max", [P, NG, TT, MAX_SLOT])
        neg_rows = sb("neg_rows", [MAX_SLOT, NG, T])
        v_cols = sb("v_cols", [P, TT, H, 32])
        probs = sb("probs", [P, 2, GH, T])
        o_cols = sb("o_cols", [P, NG, T])
        inv_sum = sb("inv_sum", [P, TT, H])
        o_rows = sb("o_rows", [P, TT, E])
        o_t = sb("o_t", [P, T])
        gated = sb("gated", [P, TT, E])
        out_sb = sb("out_sb", [P, TT, E])

        r_act = sb("r_act", [P, T])
        lg = sb("lg", [P, 10, TT, NE])
        top = sb("top", [P, 8, TT])
        gate_w = sb("gate_w", [P, TT, NE])
        gate_t = sb("gate_t", [TT * NE, P])
        eh = sb("eh", [P, EH_RING, T])
        acc = sb("acc", [P, TT, E])
        y_sum = sb("y_sum", [P, TT, E])
        g_silu = sb("g_silu", [P, TT, E])

        bank = [ctx.enter_context(nc.psum_tensor(f"bank{i}", [P, T], F32)) for i in range(4, 8)]
        ring = ctx.enter_context(nc.psum_tensor("ring", [P, 4, T], F32))
        wide = bank[0:2]
        misc = bank[2:4]

        s_att_w, s_kv_w, s_const, s_table, s_rw, s_e1, s_e2 = (
            sem(n) for n in ("s_att_w", "s_kv_w", "s_const", "s_table", "s_rw", "s_e1", "s_e2"))
        s_x0, s_x = sem("s_x0"), sem("s_x")
        prep_dve, prep_pe, prep_act = sem("prep_dve"), sem("prep_pe"), sem("prep_act")
        var_ready, rstd_ready, xn_ready = sem("var_ready"), sem("rstd_ready"), sem("xn_ready")
        x_hi_ready, x_lo_ready = sem("x_hi_ready"), sem("x_lo_ready")
        rope_ready, roped_ready = sem("rope_ready"), sem("roped_ready")
        hi_ready, lo_ready = sem("hi_ready"), sem("lo_ready")
        q_in = [sem(f"q_in{g}") for g in range(NG)]
        k_in = [sem(f"k_in{g}") for g in range(NG)]
        heads_ready = sem("heads_ready")
        max_full, max_done = sem("max_full"), sem("max_done")
        neg_ready, neg_rows_ready = sem("neg_ready"), sem("neg_rows_ready")
        neg_in = [sem(f"neg_in{g}") for g in range(NG)]
        hidden_full, hidden_done = sem("hidden_full"), sem("hidden_done")
        experts_done = sem("experts_done")
        r_ready, gap_ready, tanh_ready = sem("r_ready"), sem("gap_ready"), sem("tanh_ready")
        w_ready, wt_ready = sem("w_ready"), sem("wt_ready")
        y_ready, g_ready = sem("y_ready"), sem("g_ready")
        st_full, exp_done, pv_done, o_done = (sem(n) for n in ("st_full", "exp_done", "pv_done", "o_done"))
        v_ready = sem("v_ready")
        rows_ready, o_t_ready, gated_ready = sem("rows_ready"), sem("o_t_ready"), sem("gated_ready")
        out_ready, stored = sem("out_ready"), sem("stored")
        misc_full = sem("misc_full")
        max0_done, logits_read, acc_ready = sem("max0_done"), sem("logits_read"), sem("acc_ready")
        dve_step, pool_step, act_step = sem("dve_step"), sem("pool_step"), sem("act_step")

        read_out = {"router": (r_ready, 1), "logits": (logits_read, 1), "layer2": (acc_ready, NE),
                    "out_rows": (rows_ready, TT), "out_cols": (o_t_ready, 1), "project": (gated_ready, 1),
                    "weights_t": (wt_ready, 1), "neg_max": (neg_rows_ready, NG), "expert_bias": (y_ready, 1),
                    "x_cols": (x_lo_ready, 1), "proj": (rope_ready, 4), "values": (v_ready, 1),
                    "max0": (max0_done, NMAX0)}

        def batch_of(step, b):
            return b - 1 if step[0] in FINAL else b + 1 if step in AHEAD else b

        class Jobs:

            def __init__(self, name, b):
                self.name, self.b, self.jobs = name, b, JOBS[name]
                start = len(JOBS["prologue"])
                after_first = start + len(JOBS["first"])
                self.base = {"prologue": 0, "first": start,
                             "epilogue": after_first + (B - 2) * PER_BATCH + len(JOBS["last"]),
                             }[name] if name in ("prologue", "first", "epilogue") else (b - 1) * PER_BATCH + after_first

            def bank(self, step):
                return misc[self.jobs.index(step) % 2]

            def ordinal(self, step):
                return self.base + self.jobs.index(step) + 1

            def freed_by(self, step):
                i = self.jobs.index(step)
                if i >= 2:
                    prev, b = self.jobs[i - 2], self.b
                elif self.name == "prologue":
                    return None
                else:
                    prev, b = JOBS[BEFORE[self.name]][i - 2], self.b - 1
                who, per = read_out[prev[0]]
                return who, per * batch_of(prev, b) + prev[1] + 1

        def wait_full(eng, jobs, step):
            eng.wait_ge(misc_full, jobs.ordinal(step))
            return jobs.bank(step)

        def walk(do, steps, jobs, b):
            for step in steps:
                if step[0] in do:
                    do[step[0]](batch_of(step, b), step[1], jobs)

        def prologue(do):
            walk(do, AHEAD, Jobs("prologue", -1), -1)

        def first_round(do):
            walk(do, steps_of(first=True), Jobs("first", 0), 0)

        def middle_round(do, b):
            walk(do, steps_of(), Jobs("middle", b), b)

        def last_round(do):
            walk(do, steps_of(last=True), Jobs("last", B - 1), B - 1)
            walk(do, [s for s in STAGE_B if s[0] in FINAL], Jobs("epilogue", B), B)

        def run(eng, do):
            prologue(do)
            first_round(do)
            with eng.Fori(1, B - 1) as b:
                middle_round(do, b)
            last_round(do)

        def later(b, base):
            return not (isinstance(b, int) and b < base)

        block = ctx.enter_context(nc.Block())

        @block.sync
        def _(sp):
            tokens = x.rearrange("b (t p) e -> p b t e", p=P)
            sp.dma_start(x_all[:, 0, :, :], tokens[:, 0]).then_inc(s_x0, 16)
            sp.dma_start(ident[:], ident_c).then_inc(s_att_w, 16)
            sp.dma_start(w_in[:, 0, :], wq).then_inc(s_att_w, 16)
            sp.dma_start(w_in[:, 1, 0:L], w_down).then_inc(s_kv_w, 16)
            sp.dma_start(kv_up[:, 0:E], wk_up).then_inc(s_kv_w, 16)
            sp.dma_start(kv_up[:, E:2 * E], wv_up).then_inc(s_kv_w, 16)
            sp.dma_start(cos_sb[:], cos_t).then_inc(s_table, 16)
            sp.dma_start(sin_sb[:], sin_t).then_inc(s_table, 16)
            sp.dma_start(mask_sb[MASK0:P, :], query_rows).then_inc(s_const, 16)
            for g in range(NG):
                sp.dma_start(k_stack[MASK0:P, g, :], key_rows).then_inc(s_const, 16)
            sp.dma_start(hmask[:], head_mask).then_inc(s_const, 16)
            sp.dma_start(rank[:], rank_c.partition_broadcast(P)).then_inc(s_rw, 16)
            sp.dma_start(rb2_bc[:], rb2.partition_broadcast(P)).then_inc(s_rw, 16)
            sp.dma_start(w_in[:, 2, :], rw1).then_inc(s_rw, 16)
            sp.dma_start(w_in[:, 3, :], wo).then_inc(s_rw, 16)
            sp.dma_start(rw2_sb[:], rw2).then_inc(s_rw, 16)
            sp.dma_start(bias_rows[0:NL1, :], eb1.rearrange("e (f p) -> (e f) p", p=P)).then_inc(s_rw, 16)
            sp.dma_start(bias_rows[NL1:NL1 + 1, :], rb1.unsqueeze(0)).then_inc(s_rw, 16)
            sp.dma_start(probs[:].rearrange("p a h t -> p (a h t)")[:, 0:NE * HID].rearrange(
                "p (e h) -> p e h", e=NE), ew1.rearrange("e d h -> d e h")).then_inc(s_e1, 16)
            sp.dma_start(ew2_sb[:], ew2.rearrange("e (f p) d -> p e f d", p=P)).then_inc(s_e2, 16)
            for t in range(TT):
                sp.dma_start(x_all[:, 1:B, t, :], tokens[:, 1:B, t]).then_inc(s_x, 16)
            sp.wait_ge(prep_dve, 1)
            for t in range(TT):
                sp.dma_start(eb2_blocks[NE * t:NE * t + NE, t * E:(t + 1) * E], eb2).then_inc(s_e2, 16)

            def stack(b, g, jobs):
                if g == 0:
                    sp.wait_ge(lo_ready, 2 * b + 2)
                if later(b, 1):
                    sp.wait_ge(pv_done, NSTEP * (b - 1) + 3 * g + 2)
                    sp.wait_ge(heads_ready, NG * (b - 1) + g + 1)
                rows = slice(32 * g, 32 * g + 32)
                for slot, part in ((0, roped_hi), (1, roped_hi), (2, roped_lo)):
                    sp.dma_start(k_stack[32 * slot:32 * slot + 32, g, :],
                                 part[rows, 1, :].bitcast(F32)).then_inc(k_in[g], 16)
                for slot, part in ((0, roped_hi), (1, roped_lo), (2, roped_hi)):
                    sp.dma_start(q_stack[32 * slot:32 * slot + 32, g, :].bitcast(F32),
                                 part[rows, 0, :].bitcast(F32)).then_inc(q_in[g], 16)

            def maxima(b, g, jobs):
                sp.wait_ge(neg_rows_ready, NG * b + g + 1)
                sp.dma_start(q_stack[MAX0:MAX0 + MAX_SLOT, g, :].bitcast(F32),
                             neg_rows[:, g, :]).then_inc(neg_in[g], 16)

            def store(b, _, jobs):
                sp.wait_ge(out_ready, b + 1)
                sp.dma_start(out[b].rearrange("(t p) e -> p t e", p=P), out_sb[:]).then_inc(stored, 16)

            sp.wait_ge(prep_dve, 2)
            run(sp, {"stack": stack, "neg_max": maxima, "project": store})
            sp.wait_ge(stored, 16 * B)

        @block.tensor
        def _(pe):
            mm = nc.tensor.matmul

            pe.wait_ge(s_att_w, 32)
            pe.wait_ge(s_kv_w, 48)
            nc.tensor.transpose(wide[0][0:L, 0:E], w_in[:, 1, 0:L], ident[:]).then_inc(prep_pe, 1)
            pe.wait_ge(s_rw, 16 * 7)
            nc.tensor.transpose(wide[1][:, 0:NL1 + 1], bias_rows[:], ident[0:NL1 + 1, 0:NL1 + 1]).then_inc(prep_pe, 1)
            pe.wait_ge(prep_act, 1)
            mm(wide[0][:, 0:2 * E], wd_t[:], kv_up[:], start=True, stop=True).then_inc(prep_pe, 1)

            def take(jobs, step):
                freed = jobs.freed_by(step)
                if freed:
                    pe.wait_ge(*freed)
                return jobs.bank(step), misc_full

            def x_cols(b, n, jobs):
                pe.wait_ge(xn_ready, b + 1)
                ps, full = take(jobs, ("x_cols", n))
                for t in range(TT):
                    last = nc.tensor.transpose(ps[:, t * P:(t + 1) * P], xn[:, t, :], ident[:])
                last.then_inc(full, 1)

            def split_product(ps, w_hi, w_lo, b):
                mm(ps, w_hi, x_hi[:], start=True, stop=False)
                mm(ps, w_lo, x_hi[:], start=False, stop=False)
                return mm(ps, w_hi, x_lo[:], start=False, stop=True)

            def proj(b, n, jobs):
                if n == 0:
                    pe.wait_ge(x_hi_ready, 2 * b + 2)
                    pe.wait_ge(x_lo_ready, b + 1)
                    if isinstance(b, int) and b == 0:
                        pe.wait_ge(prep_dve, 3)
                ps, full = take(jobs, ("proj", n))
                split_product(ps[:], w_att_hi[:, n, :], w_att_lo[:, n, :], b).then_inc(full, 1)

            def values(b, n, jobs):
                ps, full = take(jobs, ("values", n))
                for t in range(TT):
                    last = mm(ps[:, t * E:(t + 1) * E], x_col[:, t * P:(t + 1) * P], w_v[:], start=True, stop=True)
                last.then_inc(full, 1)

            def router(b, n, jobs):
                if isinstance(b, int) and b == 0:
                    pe.wait_ge(prep_dve, 4)
                ps, full = take(jobs, ("router", n))
                split_product(ps[:], rw1_hi[:], rw1_lo[:], b).then_inc(full, 1)

            def logits(b, n, jobs):
                pe.wait_ge(r_ready, b + 1)
                ps, full = take(jobs, ("logits", n))
                for t in range(TT):
                    last = mm(ps[:, t * NE:(t + 1) * NE], r_act[:, t * P:(t + 1) * P], rw2_sb[:], start=True, stop=True)
                last.then_inc(full, 1)

            def layer1(b, s, jobs):
                if isinstance(b, int) and b == 0 and s == 0:
                    pe.wait_ge(prep_dve, 6)
                if s >= 2:
                    pe.wait_ge(hidden_done, NL1 * b + s - 1)
                elif later(b, 1):
                    pe.wait_ge(o_done, NG * b - 1 + s)
                e, f = divmod(s, HALVES)
                w = slice(f * P, (f + 1) * P)
                split_product(wide[s % 2][:], ew1_hi[:, e, w], ew1_lo[:, e, w], b).then_inc(hidden_full, 1)

            def layer2(b, e, jobs):
                pe.wait_ge(hidden_done, NL1 * b + HALVES * (e + 1))
                if isinstance(b, int) and b == 0 and e == 0:
                    pe.wait_ge(s_e2, 16 * (1 + TT))
                ps, full = take(jobs, ("layer2", e))
                for t in range(TT):
                    for f in range(HALVES):
                        s = HALVES * e + f
                        last = mm(ps[:, t * E:(t + 1) * E], eh[:, s % EH_RING, t * P:(t + 1) * P],
                                  ew2_sb[:, e, f, :], start=(f == 0), stop=(f == HALVES - 1))
                last.then_inc(full, 1)

            def weights_t(b, n, jobs):
                pe.wait_ge(w_ready, b + 1)
                ps, full = take(jobs, ("weights_t", n))
                nc.tensor.transpose(ps[0:TT * NE, 0:P], gate_w[:].rearrange("p t e -> p (t e)"),
                                    ident[:]).then_inc(full, 1)

            def expert_bias(b, n, jobs):
                pe.wait_ge(wt_ready, b + 1)
                ps, full = take(jobs, ("expert_bias", n))
                mm(ps[:], gate_t[:], eb2_blocks[:], start=True, stop=True).then_inc(full, 1)

            def row_scores(ps, g, i, r):
                width = max(2, i + 1) * P
                return mm(ps[:, 0:width], q_stack[0:MAX0, g, i * P:(i + 1) * P], k_head[0:MAX0, GH * g + r, 0:width],
                          start=True, stop=True)

            def max0(b, n, jobs):
                i, r = divmod(n, GH)
                if n == 0:
                    pe.wait_ge(heads_ready, NG * b + 1)
                    pe.wait_ge(q_in[0], 48 * b + 48)
                ps, full = take(jobs, ("max0", n))
                row_scores(ps, 0, i, r).then_inc(full, 1)

            def max_scores(b, m, jobs):
                g, i, pair = 1 + m // NPAIR, m % NPAIR // 2, m % 2
                if m % NPAIR == 0:
                    pe.wait_ge(heads_ready, NG * b + g + 1)
                    pe.wait_ge(q_in[g], 48 * b + 48)
                if m >= 2:
                    pe.wait_ge(max_done, NMAX * b + m - 1)
                elif later(b, 1):
                    pe.wait_ge(exp_done, NEXP * NSTEP * b)
                for r in range(2):
                    last = row_scores(ring[:, 2 * (m % 2) + r, :], g, i, 2 * pair + r)
                last.then_inc(max_full, 1)

            def neg_max_t(b, g, jobs):
                pe.wait_ge(neg_ready, NG * b + g + 1)
                ps, full = take(jobs, ("neg_max", g))
                for i in range(TT):
                    last = nc.tensor.transpose(ps[0:MAX_SLOT, i * P:(i + 1) * P], neg_max[:, g, i, :], ident[:])
                last.then_inc(full, 1)

            def scores(b, n, jobs):
                g, j = divmod(n, 3)
                if j == 0:
                    pe.wait_ge(neg_in[g], 16 * b + 16)
                if n == 0:
                    pe.wait_ge(max_done, NMAX * b + NMAX)
                for r in range(GH):
                    if n > 0 and r % 2 == 0:
                        pe.wait_ge(exp_done, NEXP * (NSTEP * b + n - 1) + r // 2 + 1)
                    h = GH * g + r
                    if j < 2:
                        mm(ring[:, r, j * P:T], k_head[:, h, j * P:(j + 1) * P], q_stack[:, g, j * P:T],
                           start=True, stop=True).then_inc(st_full, 1)
                    else:
                        mm(ring[:, r, 0:2 * P], k_head[:, h, 3 * P:T], q_stack[:, g, 2 * P:T], start=True, stop=True)
                        mm(ring[:, r, 2 * P:T], k_head[:, h, 2 * P:3 * P], q_stack[:, g, 2 * P:T],
                           start=True, stop=True).then_inc(st_full, 1)

            def pv(b, n, jobs):
                g, j = divmod(n, 3)
                if n == 0:
                    pe.wait_ge(hidden_done, NL1 * b + NL1)
                    pe.wait_ge(v_ready, b + 1)
                elif j == 0 and g >= 2:
                    pe.wait_ge(o_done, NG * b + g - 1)
                pe.wait_ge(exp_done, NEXP * (NSTEP * b + n + 1))
                parts = ((j, j * P, j * P),) if j < 2 else ((2, 2 * P, 2 * P), (3, P, 3 * P))
                for tile, src, dst in parts:
                    for r in range(GH):
                        last = mm(wide[g % 2][32 * r:32 * r + 32, dst:T], v_cols[:, tile, GH * g + r, :],
                                  probs[:, n % 2, r, src:src + T - dst], start=(tile == 0), stop=(tile == TT - 1),
                                  skip_group_check=True)
                last.then_inc(pv_done, 1)

            def out_rows(b, i, jobs):
                if i == 0:
                    pe.wait_ge(o_done, NG * b + NG)
                ps, full = take(jobs, ("out_rows", i))
                for g in range(NG):
                    last = nc.tensor.transpose(ps[:, g * P:(g + 1) * P], o_cols[:, g, i * P:(i + 1) * P], ident[:])
                last.then_inc(full, 1)

            def out_cols(b, n, jobs):
                pe.wait_ge(rows_ready, TT * b + TT)
                ps, full = take(jobs, ("out_cols", n))
                for t in range(TT):
                    last = nc.tensor.transpose(ps[:, t * P:(t + 1) * P], o_rows[:, t, :], ident[:])
                last.then_inc(full, 1)

            def project(b, n, jobs):
                pe.wait_ge(o_t_ready, b + 1)
                ps, full = take(jobs, ("project", n))
                for t in range(TT):
                    last = mm(ps[:, t * E:(t + 1) * E], o_t[:, t * P:(t + 1) * P], w_in[:, 3, :], start=True, stop=True)
                last.then_inc(full, 1)

            run(pe, {"x_cols": x_cols, "proj": proj, "values": values, "router": router, "logits": logits,
                     "layer1": layer1, "layer2": layer2, "weights_t": weights_t, "expert_bias": expert_bias,
                     "max0": max0, "max": max_scores, "neg_max": neg_max_t, "scores": scores, "pv": pv,
                     "out_rows": out_rows, "out_cols": out_cols, "project": project})

        @block.scalar
        def _(act):
            copy = nc.scalar.copy

            act.wait_ge(prep_pe, 1)
            copy(wd_t[:], wide[0][0:L, 0:E]).then_inc(prep_act, 1)

            def x_cols(b, n, jobs):
                ps = wait_full(act, jobs, ("x_cols", n))
                copy(x_hi[:], ps[:]).then_inc(x_hi_ready, 1)
                copy(x_col[:], ps[:]).then_inc(x_hi_ready, 1)

            def split(b, which, jobs):
                act.wait_ge(roped_ready, 2 * b + which + 1)
                if which == 0 and later(b, 1):
                    for g in range(NG):
                        act.wait_ge(q_in[g], 48 * b)
                        act.wait_ge(k_in[g], 48 * b)
                copy(roped_hi[:, which, :], roped[:, which, :]).then_inc(hi_ready, 1)

            def router(b, n, jobs):
                if isinstance(b, int) and b == 0:
                    act.wait_ge(prep_dve, 6)
                ps = wait_full(act, jobs, ("router", n))
                nc.scalar.activation(r_act[:], ps[:], ACT.Silu, bias=bias_cols[:, NL1:NL1 + 1]).then_inc(r_ready, 1)

            def layer1(b, s, jobs):
                act.wait_ge(hidden_full, NL1 * b + s + 1)
                if s >= EH_RING:
                    act.wait_ge(misc_full, jobs.ordinal(("layer2", (s - EH_RING) // HALVES)))
                nc.scalar.activation(eh[:, s % EH_RING, :], wide[s % 2][:], ACT.Silu,
                                     bias=bias_cols[:, s:s + 1]).then_inc(hidden_done, 1)

            def weights(b, n, jobs):
                act.wait_ge(gap_ready, b + 1)
                nc.scalar.activation(top[:, 5, :], top[:, 4, :], ACT.Tanh, scale=0.5).then_inc(tanh_ready, 1)

            def weights_t(b, n, jobs):
                ps = wait_full(act, jobs, ("weights_t", n))
                copy(gate_t[:], ps[0:TT * NE, 0:P]).then_inc(wt_ready, 1)

            def neg_max_t(b, g, jobs):
                ps = wait_full(act, jobs, ("neg_max", g))
                if later(b, 1):
                    act.wait_ge(neg_in[g], 16 * b)
                copy(neg_rows[:, g, :], ps[0:MAX_SLOT, :]).then_inc(neg_rows_ready, 1)

            def expert_bias(b, n, jobs):
                act.wait_ge(y_ready, b + 1)
                if later(b, 1):
                    act.wait_ge(gated_ready, b)
                nc.scalar.activation(g_silu[:], y_sum[:], ACT.Silu).then_inc(g_ready, 1)

            def scores(b, n, jobs):
                lo = (0, P, P)[n % 3]
                if n >= 2 or later(b, 1):
                    act.wait_ge(pv_done, NSTEP * b + n - 1)
                for r in range(0, GH, 2):
                    act.wait_ge(st_full, GH * (NSTEP * b + n) + r + 2)
                    nc.scalar.activation(probs[:, n % 2, r:r + 2, lo:T], ring[:, r:r + 2, lo:T], ACT.Exp,
                                         scale=SCALE).then_inc(exp_done, 1)

            def out_cols(b, n, jobs):
                ps = wait_full(act, jobs, ("out_cols", n))
                copy(o_t[:], ps[:]).then_inc(o_t_ready, 1)

            run(act, {"x_cols": x_cols, "split": split, "router": router, "layer1": layer1,
                      "weights": weights, "weights_t": weights_t, "neg_max": neg_max_t, "expert_bias": expert_bias,
                      "scores": scores, "out_cols": out_cols})

        @block.vector
        def _(dve):
            V = nc.vector
            tt, ts, stt = V.tensor_tensor, V.tensor_scalar, V.scalar_tensor_tensor
            steps = [0, 0]

            def link(ins):
                ins.then_inc(dve_step, 1)
                steps[0] += 1
                dve.wait_ge(dve_step, steps[1] + steps[0])

            V.memset(eb2_blocks[:], 0.0).then_inc(prep_dve, 1)
            V.memset(half_exp[:], -0.5)
            V.memset(v_cols[:], 0.0).then_inc(dve_step, 1)
            dve.wait_ge(dve_step, 1)
            dve.wait_ge(s_const, 16 * (2 + NG))
            for g in range(NG):
                V.tensor_copy(q_stack[MASK0:P, g, :], mask_sb[MASK0:P, :])
            V.memset(v_cols[:, :, :, D:D + 1], 1.0).then_inc(prep_dve, 1)
            dve.wait_ge(prep_dve, 2)
            dve.wait_ge(s_att_w, 32)
            V.tensor_copy(w_att[:, 0, :], w_in[:, 0, :])
            dve.wait_ge(prep_pe, 3)
            V.tensor_copy(w_v[:], wide[0][:, E:2 * E])
            V.tensor_copy(w_att[:, 2, :], wide[0][:, 0:E]).then_inc(dve_step, 1)
            dve.wait_ge(dve_step, 2)
            for w in (0, 2):
                pairs = w_att[:, w, :].rearrange("p (i two) -> p i two", two=2)
                turned = w_att[:, w + 1, :].rearrange("p (i two) -> p i two", two=2)
                ts(turned[:, :, 0], pairs[:, :, 1], -1.0, None, ALU.mult)
                V.tensor_copy(turned[:, :, 1], pairs[:, :, 0]).then_inc(dve_step, 1)
            dve.wait_ge(dve_step, 4)
            V.tensor_copy(w_att_hi[:], w_att[:]).then_inc(dve_step, 1)
            dve.wait_ge(dve_step, 5)
            tt(w_att_lo[:], w_att[:], w_att_hi[:].bitcast(F32), ALU.subtract).then_inc(prep_dve, 1)

            def row_stats(b, n, jobs):
                if later(b, 1):
                    dve.wait_ge(s_x, 16 * TT)
                else:
                    dve.wait_ge(s_x0, 16)
                for t in range(TT):
                    ins = V.bn_stats(stats[:, t, :], x_all[:, b, t, :])
                link(ins)
                even, odd = stats[:, :, 0:3], stats[:, :, 3:6]
                tt(mv[:, 0, :], even[:, :, 1], odd[:, :, 1], ALU.add)
                tt(mv[:, 1, :], even[:, :, 1], odd[:, :, 1], ALU.subtract)
                link(tt(mv[:, 2, :], even[:, :, 2], odd[:, :, 2], ALU.add))
                ts(mean[:], mv[:, 0, :], 0.5, None, ALU.mult)
                ts(mv[:, 3, :], mv[:, 2, :], 1.0 / E, EPS, ALU.mult, ALU.add)
                link(tt(mv[:, 4, :], mv[:, 1, :], mv[:, 1, :], ALU.mult))
                stt(out=var_eps[:], in0=mv[:, 4, :], scalar=0.25, in1=mv[:, 3, :], op0=ALU.mult,
                    op1=ALU.add).then_inc(var_ready, 1)

            def norm(b, n, jobs):
                dve.wait_ge(rstd_ready, b + 1)
                for t in range(TT):
                    ins = ts(xn[:, t, :], x_all[:, b, t, :], mean[:, t:t + 1], rstd[:, t:t + 1],
                             ALU.subtract, ALU.mult)
                ins.then_inc(xn_ready, 1)

            def x_cols(b, n, jobs):
                ps = wait_full(dve, jobs, ("x_cols", n))
                dve.wait_ge(x_hi_ready, 2 * b + 2)
                tt(x_lo[:], ps[:], x_hi[:].bitcast(F32), ALU.subtract).then_inc(x_lo_ready, 1)

            def proj(b, n, jobs):
                ps = wait_full(dve, jobs, ("proj", n))
                if isinstance(b, int) and b == 0 and n == 0:
                    dve.wait_ge(s_table, 32)
                which, term = divmod(n, 2)
                if term == 0 and later(b, 1):
                    dve.wait_ge(roped_ready, 2 * b - 1 + which)
                tt(rope_t[:, which, term, :], ps[:], (cos_sb, sin_sb)[term][:], ALU.mult).then_inc(rope_ready, 1)

            def wide4(ap):
                return ap.unsqueeze(2).to_broadcast([P, TT, NE])

            def logits(b, n, jobs):
                ps = wait_full(dve, jobs, ("logits", n))
                tt(lg[:, 0], ps[:, 0:TT * NE].rearrange("p (t e) -> p t e", e=NE),
                   rb2_bc[:].unsqueeze(1).to_broadcast([P, TT, NE]), ALU.add).then_inc(logits_read, 1)
                dve.wait_ge(logits_read, b + 1)

            def top_two(b, n, jobs):
                if n > 0:
                    dve.wait_ge(dve_step, steps[1] + steps[0])
                k, m = divmod(n, 6)
                a, eq, key, one = (lg[:, 5 * k + i] for i in range(4))
                if m == 0:
                    ins = V.tensor_reduce(top[:, k, :], a, AX, ALU.max)
                elif m == 1:
                    ins = tt(eq, a, wide4(top[:, k, :]), ALU.is_equal)
                elif m == 2:
                    ins = tt(key, eq, rank[:].unsqueeze(1).to_broadcast([P, TT, NE]), ALU.mult)
                elif m == 3:
                    ins = V.tensor_reduce(top[:, 2 + k, :], key, AX, ALU.max)
                elif m == 4:
                    ins = tt(one, key, wide4(top[:, 2 + k, :]), ALU.is_equal)
                else:
                    ins = stt(out=lg[:, 5], in0=one, scalar=-3.0e38, in1=a, op0=ALU.mult, op1=ALU.add)
                ins.then_inc(dve_step, 1)
                steps[0] += 1
                if n == NTOP - 1:
                    tt(top[:, 4, :], top[:, 1, :], top[:, 0, :], ALU.subtract).then_inc(gap_ready, 1)

            def weights(b, n, jobs):
                dve.wait_ge(tanh_ready, b + 1)
                ts(top[:, 6, :], top[:, 5, :], -0.5, 0.5, ALU.mult, ALU.add)
                link(ts(top[:, 7, :], top[:, 5, :], 0.5, 0.5, ALU.mult, ALU.add))
                tt(lg[:, 4], lg[:, 3], top[:, 6, :].unsqueeze(2).to_broadcast([P, TT, NE]), ALU.mult)
                link(tt(lg[:, 9], lg[:, 8], top[:, 7, :].unsqueeze(2).to_broadcast([P, TT, NE]), ALU.mult))
                tt(gate_w[:], lg[:, 4], lg[:, 9], ALU.add).then_inc(w_ready, 1)

            def max0(b, n, jobs):
                i, r = divmod(n, GH)
                ps = wait_full(dve, jobs, ("max0", n))
                V.tensor_reduce(row_max[:, 0, i, r:r + 1], ps[:, 0:(i + 1) * P], AX, ALU.max).then_inc(max0_done, 1)

            def max_scores(b, m, jobs):
                g, i, pair = 1 + m // NPAIR, m % NPAIR // 2, m % 2
                dve.wait_ge(max_full, NMAX * b + m + 1)
                V.tensor_reduce(row_max[:, g, i, 2 * pair:2 * pair + 2],
                                ring[:, 2 * (m % 2):2 * (m % 2) + 2, 0:(i + 1) * P], AX, ALU.max).then_inc(max_done, 1)

            def negate(b, g, jobs):
                if g == 0:
                    dve.wait_ge(max0_done, NMAX0 * b + NMAX0)
                else:
                    dve.wait_ge(max_done, NMAX * b + NPAIR * g)
                link(ts(neg_max[:, g, :, 0:GH].bitcast(F32R), row_max[:, g], -1.0, None, ALU.mult))
                stt(out=neg_max[:, g, :, GH:2 * GH].bitcast(F32R), in0=row_max[:, g], scalar=-1.0,
                    in1=neg_max[:, g, :, 0:GH], op0=ALU.mult, op1=ALU.subtract).then_inc(neg_ready, 1)

            def heads(b, g, jobs):
                if isinstance(b, int) and b == 0 and g == 0:
                    dve.wait_ge(s_const, 16 * (2 + NG))
                dve.wait_ge(k_in[g], 48 * b + 48)
                for r in range(GH):
                    last = ts(k_head[:, GH * g + r, :], k_stack[:, g, :], hmask[:, r:r + 1], None, ALU.mult)
                last.then_inc(heads_ready, 1)

            def pv(b, n, jobs):
                g, j = divmod(n, 3)
                if j == 2:
                    dve.wait_ge(pv_done, NSTEP * b + n + 1)
                    V.tensor_copy(o_cols[:, g, :], wide[g % 2][:]).then_inc(o_done, 1)

            def values(b, n, jobs):
                ps = wait_full(dve, jobs, ("values", n))
                if later(b, 1):
                    dve.wait_ge(pv_done, NSTEP * b)
                V.tensor_copy(v_cols[:, :, :, 0:D],
                              ps[:].rearrange("p (t h d) -> p t h d", t=TT, h=H)).then_inc(v_ready, 1)

            def layer2(b, e, jobs):
                ps = wait_full(dve, jobs, ("layer2", e))
                if e == 0:
                    dve.wait_ge(w_ready, b + 1)
                else:
                    dve.wait_ge(acc_ready, NE * b + e)
                for t in range(TT):
                    ins = stt(out=acc[:, t, :], in0=ps[:, t * E:(t + 1) * E], scalar=gate_w[:, t, e:e + 1],
                              in1=(xn if e == 0 else acc)[:, t, :], op0=ALU.mult, op1=ALU.add)
                ins.then_inc(acc_ready, 1)

            def expert_bias(b, n, jobs):
                ps = wait_full(dve, jobs, ("expert_bias", n))
                dve.wait_ge(acc_ready, NE * b + NE)
                tt(y_sum[:].rearrange("p t e -> p (t e)"), acc[:].rearrange("p t e -> p (t e)"), ps[:],
                   ALU.add).then_inc(y_ready, 1)

            def out_rows(b, i, jobs):
                ps = wait_full(dve, jobs, ("out_rows", i))
                cols = ps[:].rearrange("p (h c) -> p h c", h=H)
                link(V.reciprocal(inv_sum[:, i, :], cols[:, :, D]))
                tt(o_rows[:, i, :].rearrange("p (h d) -> p h d", h=H), cols[:, :, 0:D],
                   inv_sum[:, i, :].unsqueeze(2).to_broadcast([P, H, D]), ALU.mult).then_inc(rows_ready, 1)

            def project(b, n, jobs):
                ps = wait_full(dve, jobs, ("project", n))
                dve.wait_ge(g_ready, b + 1)
                if later(b, 1):
                    dve.wait_ge(out_ready, b)
                tt(gated[:].rearrange("p t e -> p (t e)"), ps[:], g_silu[:].rearrange("p t e -> p (t e)"),
                   ALU.mult).then_inc(gated_ready, 1)

            do = {"stats": row_stats, "norm": norm, "x_cols": x_cols, "proj": proj, "logits": logits,
                  "top": top_two, "weights": weights, "max0": max0, "max": max_scores, "negate": negate, "heads": heads, "pv": pv,
                  "values": values, "layer2": layer2, "expert_bias": expert_bias,
                  "out_rows": out_rows, "project": project}

            steps[0], steps[1] = 0, 5
            prologue(do)
            dve.wait_ge(s_rw, 16 * 7)
            link(V.tensor_copy(rw1_hi[:], w_in[:, 2, :]))
            tt(rw1_lo[:], w_in[:, 2, :], rw1_hi[:].bitcast(F32), ALU.subtract).then_inc(prep_dve, 1)
            e1_in = probs[:].rearrange("p a h t -> p (a h t)")[:, 0:NE * HID].rearrange("p (e h) -> p e h", e=NE)
            dve.wait_ge(s_e1, 16)
            link(V.tensor_copy(ew1_hi[:], e1_in))
            dve.wait_ge(prep_dve, 4)
            tt(ew1_lo[:], e1_in, ew1_hi[:].bitcast(F32), ALU.subtract).then_inc(prep_dve, 1)
            dve.wait_ge(prep_dve, 5)
            V.tensor_copy(bias_cols[:], wide[1][:, 0:NL1 + 1]).then_inc(prep_dve, 1)
            first_round(do)
            before = steps[0] + steps[1]
            steps[0] = 0
            with dve.Fori(1, B - 1) as b:
                steps[1] = before + (b - 1) * PER_LINKS
                middle_round(do, b)
                assert steps[0] == PER_LINKS, steps
            steps[:] = 0, before + (B - 2) * PER_LINKS
            last_round(do)

        @block.gpsimd
        def _(pool):
            G = nc.gpsimd

            def row_stats(b, n, jobs):
                pool.wait_ge(var_ready, b + 1)
                if isinstance(b, int) and b == 0:
                    pool.wait_ge(prep_dve, 2)
                if later(b, 1):
                    pool.wait_ge(xn_ready, b)
                G.tensor_tensor(rstd[:], var_eps[:], half_exp[:], ALU.pow).then_inc(rstd_ready, 1)

            def proj(b, n, jobs):
                if n % 2 == 1:
                    which = n // 2
                    pool.wait_ge(rope_ready, 4 * b + n + 1)
                    if later(b, 1):
                        pool.wait_ge(lo_ready, 2 * b)
                    G.tensor_tensor(roped[:, which, :], rope_t[:, which, 0, :], rope_t[:, which, 1, :],
                                    ALU.add).then_inc(roped_ready, 1)

            def split(b, which, jobs):
                pool.wait_ge(hi_ready, 2 * b + which + 1)
                G.tensor_tensor(roped_lo[:, which, :], roped[:, which, :], roped_hi[:, which, :].bitcast(F32),
                                ALU.subtract).then_inc(lo_ready, 1)

            def project(b, n, jobs):
                pool.wait_ge(gated_ready, b + 1)
                if later(b, 1):
                    pool.wait_ge(stored, 16 * b)
                G.tensor_tensor(out_sb[:], gated[:], x_all[:, b, :, :], ALU.add).then_inc(out_ready, 1)

            run(pool, {"stats": row_stats, "proj": proj, "split": split, "project": project})


PER_LINKS = sum({"top": 1, "weights": 2, "out_rows": 1, "stats": 3, "negate": 1}.get(s[0], 0)
                for s in STAGE_B + STAGE_C)


_INS = ["L0_attn_x", "L0_attn_wq", "L0_attn_w_down", "L0_attn_wk_up", "L0_attn_wv_up", "L0_attn_wo",
        "L0_ffn_rw1", "L0_ffn_rb1", "L0_ffn_rw2", "L0_ffn_rb2", "L0_ffn_ew1", "L0_ffn_eb1", "L0_ffn_ew2",
        "L0_ffn_eb2"]


def shape_constants():
    inv = 1.0 / 10000.0 ** (np.arange(0, D, 2, dtype=np.float32) / D)
    ang = np.outer(np.arange(T, dtype=np.float32), inv)
    spread = lambda a: np.ascontiguousarray(np.tile(np.repeat(a.T.astype(np.float32), 2, axis=0), (H, 1)))
    t = np.arange(T)
    tile, page = t // P, t % P // PAGE
    key_rows = np.zeros((P - MASK0, T), np.float32)
    query_rows = np.zeros((P - MASK0, T), np.float32)
    for j in range(TT):
        for a in range(3):
            key_rows[3 * j + a] = (tile == j) & (page > a)
            query_rows[3 * j + a] = np.where((tile == j) & (page == a), -BIG, 0.0)
    key_rows[MAX0 - MASK0:MAX0 - MASK0 + MAX_SLOT] = 1.0
    row = np.arange(P)
    head_mask = np.zeros((P, GH), np.float32)
    for r in range(GH):
        head_mask[:, r] = ((row < MASK0) & (row % 32 // D == r)) | ((row >= MASK0) & (row < MAX0)) | (
            (row >= MAX0) & (row < MAX0 + MAX_SLOT) & ((row - MAX0) % GH == r))
    return {"cos_t": spread(np.cos(ang)), "sin_t": spread(np.sin(ang)), "ident_c": np.eye(P, dtype=np.float32),
            "key_rows": key_rows, "query_rows": query_rows, "head_mask": head_mask,
            "rank_c": np.arange(NE, 0, -1).astype(np.float32)}


def kernel(**inputs):
    import concourse.bacc as bacc
    from concourse.bass_utils import run_bass_kernel_spmd

    nc = bacc.Bacc("TRN2", target_bir_lowering=False, num_devices=1)
    arrays, args = {}, []
    for name, a in [(n, np.ascontiguousarray(inputs[n])) for n in _INS] + list(shape_constants().items()):
        arrays[f"in_{name}"] = a
        args.append(nc.dram_tensor(f"in_{name}", a.shape, mybir.dt.from_np(a.dtype), kind="ExternalInput").ap())
    args.append(nc.dram_tensor("out_0", (B, T, E), F32, kind="ExternalOutput").ap())
    build(nc, *args)
    return run_bass_kernel_spmd(nc, [arrays], core_ids=[0]).results[0]["out_0"]
```

```python
from contextlib import ExitStack

import numpy as np
import concourse.bass as bass
from concourse import mybir

F32 = mybir.dt.float32
F32R = mybir.dt.float32r
ALU = mybir.AluOpType
ACT = mybir.ActivationFunctionType
AX = mybir.AxisListType.X

P = 128
B, T, E = 8, 512, 128
H, D = 16, 8
L = E // 2
PAGE = 32
NE, HID = 8, 256
TT = T // P
NG = 4
GH = H // NG
HALVES = HID // P
NL1 = NE * HALVES
NPAIR = TT * (GH // 2)
NMAX = (NG - 1) * NPAIR
NMAX0 = TT * GH
NSTEP = NG * 3
NEXP = GH // 2
SCALE = float(np.float32(1.0) / np.sqrt(np.float32(D)))
BIG = float(2.0 ** 100)
EPS = 1e-5
MASK0, MAX0 = 96, 96 + 3 * TT
DVE_GROUPS = 2
NACT = (NG - DVE_GROUPS) * GH
NTOP = 11
MAX_SLOT = 8
EH_RING = 6


def stage_b():
    maxima, top = iter(range(NMAX)), iter(range(NTOP))
    max_steps = (1, 1, 2, 2, 2, 2, 2, 2, 2, 2, 1, 2, 1, 1, 1, 0)
    layer2_at = {4: 0, 6: 1, 7: 2, 9: 3, 11: 4, 13: 5, 15: 6}
    extra = {0: [("logits", 0)], 1: [("gate", 0)], 2: [("out_rows", 0)], 3: [("tanh", 0), ("out_rows", 1)],
             4: [("weights", 0), ("neg_max", 0)], 5: [("out_rows", 2), ("negate", 1)],
             6: [("weights_t", 0)], 7: [("out_rows", 3)], 8: [("neg_max", 1), ("stats", 0)], 9: [("out_cols", 0)],
             10: [("negate", 2)], 11: [("project", 0)], 12: [("neg_max", 2), ("norm", 0)],
             15: [("negate", 3)]}
    seq = [("router", 0)]
    for s in range(NL1):
        seq.append(("layer1", s))
        if s == NL1 - 1:
            seq += [("x_cols", 0), ("exp_table", 0)]
        for _ in range(max_steps[s]):
            seq.append(("max", next(maxima)))
            if s >= 1:
                seq += [("top", n) for _, n in zip(range(3), top)]
        seq += extra.get(s, [])
        if s < NACT:
            seq.append(("act_head", s))
        if s in layer2_at:
            seq.append(("layer2", layer2_at[s]))
    assert not list(maxima) and not list(top)
    return seq + [("layer2", NE - 1), ("neg_max", 3), ("proj", 0), ("expert_bias", 0), ("proj", 1)]


def stage_c():
    before_pv = {5: [("heads", 0)], 8: [("heads", 1)]}
    after_pv = {0: [("proj", 2), ("split", 0), ("proj", 3)], 1: [("split", 1), ("stack", 0)], 4: [("stack", 1)],
                7: [("stack", 2)], 10: [("stack", 3)], NSTEP: [("values", 0), ("negate", 0)]}
    for n in range(NMAX0):
        at = 6 + n * 6 // NMAX0
        (after_pv if n * 6 % NMAX0 >= 12 or at == 8 else before_pv).setdefault(at, []).append(("max0", n))
    seq = []
    for n in range(NSTEP + 1):
        if n < NSTEP:
            seq.append(("scores", n))
        seq += before_pv.get(n, [])
        if n >= 1:
            seq.append(("pv", n - 1))
        seq += after_pv.get(n, [])
    return seq


STAGE_B, STAGE_C = stage_b(), stage_c()
FINAL = ("gate", "out_rows", "out_cols", "project")
AHEAD = [s for s in STAGE_B if s[0] in ("stats", "norm", "x_cols", "proj")] + [
    s for s in STAGE_C if s[0] in ("proj", "split", "stack", "values", "heads", "max0", "negate")]
MISC = ("router", "logits", "layer2", "out_rows", "out_cols", "project", "weights_t", "neg_max",
        "expert_bias", "x_cols", "proj", "values", "max0")


def opening():
    seq = [s for s in AHEAD if s[0] in ("stats", "norm", "x_cols", "proj", "values")]
    seq += [("split", 0), ("split", 1), ("stack", 0), ("stack", 1), ("stack", 2), ("stack", 3), ("router", 0),
            ("layer1", 0), ("layer1", 1), ("logits", 0)]
    top = iter(range(NTOP))
    seq += [("top", n) for _, n in zip(range(5), top)] + [("heads", 0)]
    for n in range(NMAX0):
        seq.append(("max0", n))
        if n in (3, 7):
            seq.append(("layer1", 2 + n // 4))
        if n == 7:
            seq.append(("heads", 1))
        if n >= 8:
            seq += [("top", n) for _, n in zip(range(1), top)]
    return seq + [("negate", 0)]


OPENING = opening()


def steps_of(first=False, last=False):
    return [s for s in STAGE_B + STAGE_C
            if not (first and (s[0] in FINAL or s in OPENING and s not in AHEAD)) and not (last and s in AHEAD)]


def misc_jobs(steps):
    jobs = [s for s in steps if s[0] in MISC]
    assert len(jobs) % 2 == 0
    return jobs


JOBS = {name: misc_jobs(steps) for name, steps in (
    ("prologue", OPENING), ("first", steps_of(first=True)), ("middle", steps_of()),
    ("last", steps_of(last=True)), ("epilogue", [s for s in STAGE_B if s[0] in FINAL]))}
PER_BATCH = len(JOBS["middle"])
BEFORE = {"first": "prologue", "middle": "middle", "last": "middle", "epilogue": "last"}
assert JOBS["first"][-2:] == JOBS["middle"][-2:]


def build(nc, x, wq, w_down, wk_up, wv_up, wo, rw1, rb1, rw2, rb2, ew1, eb1, ew2, eb2,
          cos_t, sin_t, ident_c, key_rows, query_rows, head_mask, rank_c, out):
    ctx = ExitStack()
    with ctx:
        def sb(name, shape, dt=F32):
            return ctx.enter_context(nc.sbuf_tensor(name, shape, dt))

        def sem(name):
            return ctx.enter_context(nc.semaphore(name))

        w_in = sb("w_in", [P, 5, E])
        kv_up = sb("kv_up", [L, 2 * E])
        wd_t = sb("wd_t", [L, E])
        w_att = sb("w_att", [P, 4, E])
        w_att_hi = sb("w_att_hi", [P, 4, E], F32R)
        w_att_lo = sb("w_att_lo", [P, 4, E], F32R)
        w_v = sb("w_v", [P, E])
        rw1_hi = sb("rw1_hi", [P, E], F32R)
        rw1_lo = sb("rw1_lo", [P, E], F32R)
        rw2_sb = sb("rw2_sb", [P, NE])
        rb2_bc = sb("rb2_bc", [P, NE])
        ew1_hi = sb("ew1_hi", [P, NE, HID], F32R)
        ew1_lo = sb("ew1_lo", [P, NE, HID], F32R)
        ew2_sb = sb("ew2_sb", [P, NE, HALVES, E])
        bias_rows = sb("bias_rows", [NL1 + 1, P])
        bias_cols = sb("bias_cols", [P, NL1 + 1])
        eb2_blocks = sb("eb2_blocks", [TT * NE, TT * E])
        cos_sb = sb("cos_sb", [P, T])
        sin_sb = sb("sin_sb", [P, T])
        ident = sb("ident", [P, P])
        mask_sb = sb("mask_sb", [P, T])
        hmask = sb("hmask", [P, GH])
        rank = sb("rank", [P, NE])
        half_exp = sb("half_exp", [P, TT])
        table_in = sb("table_in", [P, 1])
        table_out = sb("table_out", [P, 1])

        x_all = sb("x_all", [P, B, TT, E])
        xn = sb("xn", [P, TT, E])
        x_hi = sb("x_hi", [P, T], F32R)
        x_lo = sb("x_lo", [P, T], F32R)
        x_col = sb("x_col", [P, T])
        stats = sb("stats", [P, TT, 6])
        mv = sb("mv", [P, 5, TT])
        mean = sb("mean", [P, TT])
        var_eps = sb("var_eps", [P, TT])
        rstd = sb("rstd", [P, TT])

        rope_t = sb("rope_t", [P, 2, 2, T])
        roped = rope_t[:, :, 0, :]
        roped_hi = sb("roped_hi", [P, 2, T], F32R)
        roped_lo = sb("roped_lo", [P, 2, T], F32R)
        q_stack = sb("q_stack", [P, NG, T], F32R)
        k_stack = sb("k_stack", [P, NG, T])
        k_head = sb("k_head", [P, H, T], F32R)
        row_max = sb("row_max", [P, NG, TT, GH])
        neg_max = sb("neg_max", [P, NG, TT, MAX_SLOT])
        neg_rows = sb("neg_rows", [MAX_SLOT, NG, T])
        v_cols = sb("v_cols", [P, TT, H, 32])
        probs = sb("probs", [P, 2, GH, T])
        o_cols = sb("o_cols", [P, NG, T])
        inv_sum = sb("inv_sum", [P, TT, H])
        o_rows = sb("o_rows", [P, TT, E])
        o_t = sb("o_t", [P, T])
        gated = sb("gated", [P, TT, E])
        out_sb = sb("out_sb", [P, TT, E])

        r_act = sb("r_act", [P, T])
        lg = sb("lg", [P, 10, TT, NE])
        top = sb("top", [P, 8, TT])
        gate_w = sb("gate_w", [P, TT, NE])
        gate_t = sb("gate_t", [TT * NE, P])
        eh = sb("eh", [P, EH_RING, T])
        acc = sb("acc", [P, TT, E])
        y_sum = sb("y_sum", [P, TT, E])
        g_silu = sb("g_silu", [P, TT, E])

        bank = [ctx.enter_context(nc.psum_tensor(f"bank{i}", [P, T], F32)) for i in range(4, 8)]
        ring = ctx.enter_context(nc.psum_tensor("ring", [P, 4, T], F32))
        wide = bank[0:2]
        misc = bank[2:4]

        s_att_w, s_kv_w, s_const, s_table, s_rw, s_e1, s_e2 = (
            sem(n) for n in ("s_att_w", "s_kv_w", "s_const", "s_table", "s_rw", "s_e1", "s_e2"))
        s_x0, s_x = sem("s_x0"), sem("s_x")
        prep_dve, prep_pe, prep_act = sem("prep_dve"), sem("prep_pe"), sem("prep_act")
        var_ready, rstd_ready, xn_ready = sem("var_ready"), sem("rstd_ready"), sem("xn_ready")
        x_hi_ready, x_lo_ready = sem("x_hi_ready"), sem("x_lo_ready")
        rope_ready, roped_ready = sem("rope_ready"), sem("roped_ready")
        hi_ready, lo_ready = sem("hi_ready"), sem("lo_ready")
        q_in = [sem(f"q_in{g}") for g in range(NG)]
        k_in = [sem(f"k_in{g}") for g in range(NG)]
        heads_ready, act_heads_ready = sem("heads_ready"), sem("act_heads_ready")
        max_full, max_done = sem("max_full"), sem("max_done")
        neg_ready, neg_rows_ready = sem("neg_ready"), sem("neg_rows_ready")
        neg_in = [sem(f"neg_in{g}") for g in range(NG)]
        hidden_full, hidden_done = sem("hidden_full"), sem("hidden_done")
        experts_done = sem("experts_done")
        r_ready, gap_ready, tanh_ready = sem("r_ready"), sem("gap_ready"), sem("tanh_ready")
        w_ready, wt_ready = sem("w_ready"), sem("wt_ready")
        y_ready, g_ready = sem("y_ready"), sem("g_ready")
        st_full, exp_done, pv_done, o_done = (sem(n) for n in ("st_full", "exp_done", "pv_done", "o_done"))
        v_ready = sem("v_ready")
        rows_ready, o_t_ready, gated_ready = sem("rows_ready"), sem("o_t_ready"), sem("gated_ready")
        out_ready, stored = sem("out_ready"), sem("stored")
        misc_full = sem("misc_full")
        max0_done, logits_read, acc_ready = sem("max0_done"), sem("logits_read"), sem("acc_ready")
        dve_step, pool_step, act_step = sem("dve_step"), sem("pool_step"), sem("act_step")

        read_out = {"router": (r_ready, 1), "logits": (logits_read, 1), "layer2": (acc_ready, NE),
                    "out_rows": (rows_ready, TT), "out_cols": (o_t_ready, 1), "project": (gated_ready, 1),
                    "weights_t": (wt_ready, 1), "neg_max": (neg_rows_ready, NG), "expert_bias": (y_ready, 1),
                    "x_cols": (x_lo_ready, 1), "proj": (rope_ready, 4), "values": (v_ready, 1),
                    "max0": (max0_done, NMAX0)}

        def batch_of(step, b):
            return b - 1 if step[0] in FINAL else b + 1 if step in AHEAD else b

        class Jobs:

            def __init__(self, name, b):
                self.name, self.b, self.jobs = name, b, JOBS[name]
                start = len(JOBS["prologue"])
                after_first = start + len(JOBS["first"])
                self.base = {"prologue": 0, "first": start,
                             "epilogue": after_first + (B - 2) * PER_BATCH + len(JOBS["last"]),
                             }[name] if name in ("prologue", "first", "epilogue") else (b - 1) * PER_BATCH + after_first

            def bank(self, step):
                return misc[self.jobs.index(step) % 2]

            def ordinal(self, step):
                return self.base + self.jobs.index(step) + 1

            def freed_by(self, step):
                i = self.jobs.index(step)
                if i >= 2:
                    prev, b = self.jobs[i - 2], self.b
                elif self.name == "prologue":
                    return None
                else:
                    prev, b = JOBS[BEFORE[self.name]][i - 2], self.b - 1
                who, per = read_out[prev[0]]
                batch = 0 if self.name in ("prologue", "first") and i < 2 or self.name == "prologue" else batch_of(prev, b)
                return who, per * batch + prev[1] + 1

        prologue_jobs = Jobs("prologue", 0)

        def wait_full(eng, jobs, step):
            eng.wait_ge(misc_full, jobs.ordinal(step))
            return jobs.bank(step)

        def walk(do, steps, jobs, b):
            for step in steps:
                if step[0] in do:
                    do[step[0]](batch_of(step, b), step[1], jobs)

        def prologue(do):
            for name, n in OPENING:
                if name in do:
                    do[name](0, n, prologue_jobs)

        def first_round(do):
            walk(do, steps_of(first=True), Jobs("first", 0), 0)

        def middle_round(do, b):
            walk(do, steps_of(), Jobs("middle", b), b)

        def last_round(do):
            walk(do, steps_of(last=True), Jobs("last", B - 1), B - 1)
            walk(do, [s for s in STAGE_B if s[0] in FINAL], Jobs("epilogue", B), B)

        def run(eng, do):
            prologue(do)
            first_round(do)
            with eng.Fori(1, B - 1) as b:
                middle_round(do, b)
            last_round(do)

        def later(b, base):
            return not (isinstance(b, int) and b < base)

        block = ctx.enter_context(nc.Block())

        @block.sync
        def _(sp):
            tokens = x.rearrange("b (t p) e -> p b t e", p=P)
            sp.dma_start(x_all[:, 0, :, :], tokens[:, 0]).then_inc(s_x0, 16)
            sp.dma_start(ident[:], ident_c).then_inc(s_att_w, 16)
            sp.dma_start(w_in[:, 0, :], wq).then_inc(s_att_w, 16)
            sp.dma_start(w_in[:, 1, 0:L], w_down).then_inc(s_kv_w, 16)
            sp.dma_start(kv_up[:, 0:E], wk_up).then_inc(s_kv_w, 16)
            sp.dma_start(kv_up[:, E:2 * E], wv_up).then_inc(s_kv_w, 16)
            sp.dma_start(cos_sb[:], cos_t).then_inc(s_table, 16)
            sp.dma_start(sin_sb[:], sin_t).then_inc(s_table, 16)
            sp.dma_start(mask_sb[MASK0:P, :], query_rows).then_inc(s_const, 16)
            for g in range(NG):
                sp.dma_start(k_stack[MASK0:P, g, :], key_rows).then_inc(s_const, 16)
            sp.dma_start(hmask[:], head_mask).then_inc(s_const, 16)
            sp.dma_start(rank[:], rank_c.partition_broadcast(P)).then_inc(s_rw, 16)
            sp.dma_start(rb2_bc[:], rb2.partition_broadcast(P)).then_inc(s_rw, 16)
            sp.dma_start(w_in[:, 2, :], rw1).then_inc(s_rw, 16)
            sp.dma_start(w_in[:, 3, :], wo).then_inc(s_rw, 16)
            sp.dma_start(rw2_sb[:], rw2).then_inc(s_rw, 16)
            sp.dma_start(bias_rows[0:NL1, :], eb1.rearrange("e (f p) -> (e f) p", p=P)).then_inc(s_rw, 16)
            sp.dma_start(bias_rows[NL1:NL1 + 1, :], rb1.unsqueeze(0)).then_inc(s_rw, 16)
            sp.dma_start(probs[:].rearrange("p a h t -> p (a h t)")[:, 0:NE * HID].rearrange(
                "p (e h) -> p e h", e=NE), ew1.rearrange("e d h -> d e h")).then_inc(s_e1, 16)
            sp.dma_start(ew2_sb[:], ew2.rearrange("e (f p) d -> p e f d", p=P)).then_inc(s_e2, 16)
            for t in range(TT):
                sp.dma_start(x_all[:, 1:B, t, :], tokens[:, 1:B, t]).then_inc(s_x, 16)
            sp.wait_ge(prep_dve, 1)
            for t in range(TT):
                sp.dma_start(eb2_blocks[NE * t:NE * t + NE, t * E:(t + 1) * E], eb2).then_inc(s_e2, 16)

            def stack(b, g, jobs):
                parts, used = 2 * b + 2, NSTEP * (b - 1) + 3 * g + 2
                if g == 0:
                    sp.wait_ge(hi_ready, parts)
                if later(b, 1):
                    sp.wait_ge(pv_done, used)
                rows = slice(32 * g, 32 * g + 32)
                for slot in (0, 1):
                    sp.dma_start(k_stack[32 * slot:32 * slot + 32, g, :],
                                 roped_hi[rows, 1, :].bitcast(F32)).then_inc(k_in[g], 16)
                for slot in (0, 2):
                    sp.dma_start(q_stack[32 * slot:32 * slot + 32, g, :].bitcast(F32),
                                 roped_hi[rows, 0, :].bitcast(F32)).then_inc(q_in[g], 16)
                if g == 0:
                    sp.wait_ge(lo_ready, parts)
                sp.dma_start(k_stack[64:96, g, :], roped_lo[rows, 1, :].bitcast(F32)).then_inc(k_in[g], 16)
                sp.dma_start(q_stack[32:64, g, :].bitcast(F32),
                             roped_lo[rows, 0, :].bitcast(F32)).then_inc(q_in[g], 16)

            def maxima(b, g, jobs):
                sp.wait_ge(neg_rows_ready, NG * b + g + 1)
                sp.dma_start(q_stack[MAX0:MAX0 + MAX_SLOT, g, :].bitcast(F32),
                             neg_rows[:, g, :]).then_inc(neg_in[g], 16)

            def store(b, _, jobs):
                sp.wait_ge(out_ready, b + 1)
                sp.dma_start(out[b].rearrange("(t p) e -> p t e", p=P), out_sb[:]).then_inc(stored, 16)

            sp.wait_ge(prep_dve, 2)
            run(sp, {"stack": stack, "neg_max": maxima, "project": store})
            sp.wait_ge(stored, 16 * B)

        @block.tensor
        def _(pe):
            mm = nc.tensor.matmul

            pe.wait_ge(s_att_w, 32)
            pe.wait_ge(s_kv_w, 48)
            nc.tensor.transpose(wide[0][0:L, 0:E], w_in[:, 1, 0:L], ident[:]).then_inc(prep_pe, 1)
            pe.wait_ge(prep_act, 1)
            mm(wide[0][:, 0:2 * E], wd_t[:], kv_up[:], start=True, stop=True).then_inc(prep_pe, 1)

            def take(jobs, step):
                freed = jobs.freed_by(step)
                if freed:
                    pe.wait_ge(*freed)
                return jobs.bank(step), misc_full

            def x_cols(b, n, jobs):
                pe.wait_ge(xn_ready, b + 1)
                ps, full = take(jobs, ("x_cols", n))
                for t in range(TT):
                    last = nc.tensor.transpose(ps[:, t * P:(t + 1) * P], xn[:, t, :], ident[:])
                last.then_inc(full, 1)

            def split_product(ps, w_hi, w_lo, b):
                mm(ps, w_hi, x_hi[:], start=True, stop=False)
                mm(ps, w_lo, x_hi[:], start=False, stop=False)
                return mm(ps, w_hi, x_lo[:], start=False, stop=True)

            def proj(b, n, jobs):
                if n == 0:
                    pe.wait_ge(x_hi_ready, 2 * b + 2)
                    pe.wait_ge(x_lo_ready, b + 1)
                    if isinstance(b, int) and b == 0:
                        pe.wait_ge(prep_dve, 3)
                ps, full = take(jobs, ("proj", n))
                split_product(ps[:], w_att_hi[:, n, :], w_att_lo[:, n, :], b).then_inc(full, 1)

            def values(b, n, jobs):
                ps, full = take(jobs, ("values", n))
                for t in range(TT):
                    last = mm(ps[:, t * E:(t + 1) * E], x_col[:, t * P:(t + 1) * P], w_v[:], start=True, stop=True)
                last.then_inc(full, 1)

            def router(b, n, jobs):
                if isinstance(b, int) and b == 0:
                    pe.wait_ge(s_rw, 16 * 7)
                    nc.tensor.transpose(wide[1][:, 0:NL1 + 1], bias_rows[:],
                                        ident[0:NL1 + 1, 0:NL1 + 1]).then_inc(prep_pe, 1)
                    pe.wait_ge(prep_dve, 4)
                ps, full = take(jobs, ("router", n))
                split_product(ps[:], rw1_hi[:], rw1_lo[:], b).then_inc(full, 1)

            def logits(b, n, jobs):
                pe.wait_ge(r_ready, b + 1)
                ps, full = take(jobs, ("logits", n))
                for t in range(TT):
                    last = mm(ps[:, t * NE:(t + 1) * NE], r_act[:, t * P:(t + 1) * P], rw2_sb[:], start=True, stop=True)
                last.then_inc(full, 1)

            def layer1(b, s, jobs):
                if isinstance(b, int) and b == 0 and s == 0:
                    pe.wait_ge(prep_dve, 6)
                if s >= 2:
                    pe.wait_ge(hidden_done, NL1 * b + s - 1)
                elif later(b, 1):
                    pe.wait_ge(o_done, NG * b - 1 + s)
                e, f = divmod(s, HALVES)
                w = slice(f * P, (f + 1) * P)
                split_product(wide[s % 2][:], ew1_hi[:, e, w], ew1_lo[:, e, w], b).then_inc(hidden_full, 1)

            def layer2(b, e, jobs):
                pe.wait_ge(hidden_done, NL1 * b + HALVES * (e + 1))
                if isinstance(b, int) and b == 0 and e == 0:
                    pe.wait_ge(s_e2, 16 * (1 + TT))
                ps, full = take(jobs, ("layer2", e))
                for t in range(TT):
                    for f in range(HALVES):
                        s = HALVES * e + f
                        last = mm(ps[:, t * E:(t + 1) * E], eh[:, s % EH_RING, t * P:(t + 1) * P],
                                  ew2_sb[:, e, f, :], start=(f == 0), stop=(f == HALVES - 1))
                last.then_inc(full, 1)

            def weights_t(b, n, jobs):
                pe.wait_ge(w_ready, b + 1)
                ps, full = take(jobs, ("weights_t", n))
                nc.tensor.transpose(ps[0:TT * NE, 0:P], gate_w[:].rearrange("p t e -> p (t e)"),
                                    ident[:]).then_inc(full, 1)

            def expert_bias(b, n, jobs):
                pe.wait_ge(wt_ready, b + 1)
                ps, full = take(jobs, ("expert_bias", n))
                mm(ps[:], gate_t[:], eb2_blocks[:], start=True, stop=True).then_inc(full, 1)

            def row_scores(ps, g, i, r):
                width = max(2, i + 1) * P
                return mm(ps[:, 0:width], q_stack[0:MAX0, g, i * P:(i + 1) * P], k_head[0:MAX0, GH * g + r, 0:width],
                          start=True, stop=True)

            def max0(b, n, jobs):
                i, r = divmod(n, GH)
                if n == 0:
                    pe.wait_ge(heads_ready, DVE_GROUPS * b + 1)
                    pe.wait_ge(q_in[0], 48 * b + 48)
                ps, full = take(jobs, ("max0", n))
                row_scores(ps, 0, i, r).then_inc(full, 1)

            def max_scores(b, m, jobs):
                g, i, pair = 1 + m // NPAIR, m % NPAIR // 2, m % 2
                if m % NPAIR == 0:
                    pe.wait_ge(q_in[g], 48 * b + 48)
                    if g < DVE_GROUPS:
                        pe.wait_ge(heads_ready, DVE_GROUPS * b + g + 1)
                if g >= DVE_GROUPS and i == 0:
                    pe.wait_ge(act_heads_ready, NACT * b + (g - DVE_GROUPS) * GH + 2 * pair + 2)
                if m >= 2:
                    pe.wait_ge(max_done, NMAX * b + m - 1)
                elif later(b, 1):
                    pe.wait_ge(exp_done, NEXP * NSTEP * b)
                for r in range(2):
                    last = row_scores(ring[:, 2 * (m % 2) + r, :], g, i, 2 * pair + r)
                last.then_inc(max_full, 1)

            def neg_max_t(b, g, jobs):
                pe.wait_ge(neg_ready, NG * b + g + 1)
                ps, full = take(jobs, ("neg_max", g))
                for i in range(TT):
                    last = nc.tensor.transpose(ps[0:MAX_SLOT, i * P:(i + 1) * P], neg_max[:, g, i, :], ident[:])
                last.then_inc(full, 1)

            def scores(b, n, jobs):
                g, j = divmod(n, 3)
                if j == 0:
                    pe.wait_ge(neg_in[g], 16 * b + 16)
                if n == 0:
                    pe.wait_ge(max_done, NMAX * b + NMAX)
                for r in range(GH):
                    if n > 0 and r % 2 == 0:
                        pe.wait_ge(exp_done, NEXP * (NSTEP * b + n - 1) + r // 2 + 1)
                    h = GH * g + r
                    if j < 2:
                        mm(ring[:, r, j * P:T], k_head[:, h, j * P:(j + 1) * P], q_stack[:, g, j * P:T],
                           start=True, stop=True).then_inc(st_full, 1)
                    else:
                        mm(ring[:, r, 0:2 * P], k_head[:, h, 3 * P:T], q_stack[:, g, 2 * P:T], start=True, stop=True)
                        mm(ring[:, r, 2 * P:T], k_head[:, h, 2 * P:3 * P], q_stack[:, g, 2 * P:T],
                           start=True, stop=True).then_inc(st_full, 1)

            def pv(b, n, jobs):
                g, j = divmod(n, 3)
                if n == 0:
                    pe.wait_ge(hidden_done, NL1 * b + NL1)
                    pe.wait_ge(v_ready, b + 1)
                elif j == 0 and g >= 2:
                    pe.wait_ge(o_done, NG * b + g - 1)
                pe.wait_ge(exp_done, NEXP * (NSTEP * b + n + 1))
                parts = ((j, j * P, j * P),) if j < 2 else ((2, 2 * P, 2 * P), (3, P, 3 * P))
                for tile, src, dst in parts:
                    for r in range(GH):
                        last = mm(wide[g % 2][32 * r:32 * r + 32, dst:T], v_cols[:, tile, GH * g + r, :],
                                  probs[:, n % 2, r, src:src + T - dst], start=(tile == 0), stop=(tile == TT - 1),
                                  skip_group_check=True)
                last.then_inc(pv_done, 1)

            def out_rows(b, i, jobs):
                if i == 0:
                    pe.wait_ge(o_done, NG * b + NG)
                ps, full = take(jobs, ("out_rows", i))
                for g in range(NG):
                    last = nc.tensor.transpose(ps[:, g * P:(g + 1) * P], o_cols[:, g, i * P:(i + 1) * P], ident[:])
                last.then_inc(full, 1)

            def out_cols(b, n, jobs):
                pe.wait_ge(rows_ready, TT * b + TT)
                ps, full = take(jobs, ("out_cols", n))
                for t in range(TT):
                    last = nc.tensor.transpose(ps[:, t * P:(t + 1) * P], o_rows[:, t, :], ident[:])
                last.then_inc(full, 1)

            def project(b, n, jobs):
                pe.wait_ge(o_t_ready, b + 1)
                ps, full = take(jobs, ("project", n))
                for t in range(TT):
                    last = mm(ps[:, t * E:(t + 1) * E], o_t[:, t * P:(t + 1) * P], w_in[:, 3, :], start=True, stop=True)
                last.then_inc(full, 1)

            run(pe, {"x_cols": x_cols, "proj": proj, "values": values, "router": router, "logits": logits,
                     "layer1": layer1, "layer2": layer2, "weights_t": weights_t, "expert_bias": expert_bias,
                     "max0": max0, "max": max_scores, "neg_max": neg_max_t, "scores": scores, "pv": pv,
                     "out_rows": out_rows, "out_cols": out_cols, "project": project})

        @block.scalar
        def _(act):
            copy = nc.scalar.copy

            def load_table(b, n, func):
                if n > 0 or later(b, 1):
                    act.wait_ge(act_step, 2 * b + n)
                nc.scalar.activation(table_out[:], table_in[:], func).then_inc(act_step, 1)

            act.wait_ge(prep_pe, 1)
            copy(wd_t[:], wide[0][0:L, 0:E]).then_inc(prep_act, 1)

            def x_cols(b, n, jobs):
                ps = wait_full(act, jobs, ("x_cols", n))
                copy(x_hi[:], ps[:]).then_inc(x_hi_ready, 1)
                copy(x_col[:], ps[:]).then_inc(x_hi_ready, 1)

            def router(b, n, jobs):
                if isinstance(b, int) and b == 0:
                    act.wait_ge(prep_dve, 6)
                load_table(b, 0, ACT.Silu)
                ps = wait_full(act, jobs, ("router", n))
                nc.scalar.activation(r_act[:], ps[:], ACT.Silu, bias=bias_cols[:, NL1:NL1 + 1]).then_inc(r_ready, 1)

            def layer1(b, s, jobs):
                act.wait_ge(hidden_full, NL1 * b + s + 1)
                if s >= EH_RING:
                    act.wait_ge(misc_full, jobs.ordinal(("layer2", (s - EH_RING) // HALVES)))
                nc.scalar.activation(eh[:, s % EH_RING, :], wide[s % 2][:], ACT.Silu,
                                     bias=bias_cols[:, s:s + 1]).then_inc(hidden_done, 1)

            def tanh(b, n, jobs):
                act.wait_ge(gap_ready, b + 1)
                nc.scalar.activation(top[:, 5, :], top[:, 4, :], ACT.Tanh, scale=0.5).then_inc(tanh_ready, 1)

            def weights_t(b, n, jobs):
                ps = wait_full(act, jobs, ("weights_t", n))
                copy(gate_t[:], ps[0:TT * NE, 0:P]).then_inc(wt_ready, 1)

            def neg_max_t(b, g, jobs):
                ps = wait_full(act, jobs, ("neg_max", g))
                if later(b, 1):
                    act.wait_ge(neg_in[g], 16 * b)
                copy(neg_rows[:, g, :], ps[0:MAX_SLOT, :]).then_inc(neg_rows_ready, 1)

            def exp_table(b, n, jobs):
                load_table(b, 1, ACT.Exp)

            def act_head(b, n, jobs):
                g, r = DVE_GROUPS + n // GH, n % GH
                if r == 0:
                    act.wait_ge(k_in[g], 48 * b + 48)
                nc.scalar.activation(k_head[:, GH * g + r, :], k_stack[:, g, :], ACT.Copy,
                                     scale=hmask[:, r:r + 1]).then_inc(act_heads_ready, 1)

            def gate(b, n, jobs):
                act.wait_ge(y_ready, b + 1)
                if later(b, 1):
                    act.wait_ge(gated_ready, b)
                nc.scalar.activation(g_silu[:], y_sum[:], ACT.Silu).then_inc(g_ready, 1)

            def scores(b, n, jobs):
                lo = (0, P, P)[n % 3]
                if n >= 2 or later(b, 1):
                    act.wait_ge(pv_done, NSTEP * b + n - 1)
                for r in range(0, GH, 2):
                    act.wait_ge(st_full, GH * (NSTEP * b + n) + r + 2)
                    nc.scalar.activation(probs[:, n % 2, r:r + 2, lo:T], ring[:, r:r + 2, lo:T], ACT.Exp,
                                         scale=SCALE).then_inc(exp_done, 1)

            def out_cols(b, n, jobs):
                ps = wait_full(act, jobs, ("out_cols", n))
                copy(o_t[:], ps[:]).then_inc(o_t_ready, 1)

            run(act, {"x_cols": x_cols, "router": router, "layer1": layer1, "tanh": tanh,
                       "weights_t": weights_t, "neg_max": neg_max_t, "gate": gate,
                      "exp_table": exp_table, "act_head": act_head, "scores": scores, "out_cols": out_cols})

        @block.vector
        def _(dve):
            V = nc.vector
            tt, ts, stt = V.tensor_tensor, V.tensor_scalar, V.scalar_tensor_tensor
            steps = [0, 0]

            def link(ins):
                ins.then_inc(dve_step, 1)
                steps[0] += 1
                dve.wait_ge(dve_step, steps[1] + steps[0])

            V.memset(half_exp[:], -0.5)
            V.memset(table_in[:], 0.0)
            V.memset(eb2_blocks[:], 0.0).then_inc(prep_dve, 1)
            V.memset(v_cols[:], 0.0).then_inc(dve_step, 1)
            steps[1] = 1

            def attention_weights():
                dve.wait_ge(s_att_w, 32)
                V.tensor_copy(w_att[:, 0, :], w_in[:, 0, :])
                dve.wait_ge(prep_pe, 2)
                V.tensor_copy(w_v[:], wide[0][:, E:2 * E])
                link(V.tensor_copy(w_att[:, 2, :], wide[0][:, 0:E]))
                for w in (0, 2):
                    pairs = w_att[:, w, :].rearrange("p (i two) -> p i two", two=2)
                    turned = w_att[:, w + 1, :].rearrange("p (i two) -> p i two", two=2)
                    ts(turned[:, :, 0], pairs[:, :, 1], -1.0, None, ALU.mult)
                    ins = V.tensor_copy(turned[:, :, 1], pairs[:, :, 0])
                link(ins)
                link(V.tensor_copy(w_att_hi[:], w_att[:]))
                dve.wait_ge(prep_dve, 2)
                tt(w_att_lo[:], w_att[:], w_att_hi[:].bitcast(F32), ALU.subtract).then_inc(prep_dve, 1)

            def constant_rows():
                dve.wait_ge(s_const, 16 * (2 + NG))
                for g in range(NG):
                    V.tensor_copy(q_stack[MASK0:P, g, :], mask_sb[MASK0:P, :])
                V.memset(v_cols[:, :, :, D:D + 1], 1.0).then_inc(prep_dve, 1)

            def ffn_weights():
                dve.wait_ge(s_rw, 16 * 7)
                link(V.tensor_copy(rw1_hi[:], w_in[:, 2, :]))
                tt(rw1_lo[:], w_in[:, 2, :], rw1_hi[:].bitcast(F32), ALU.subtract).then_inc(prep_dve, 1)
                e1_in = probs[:].rearrange("p a h t -> p (a h t)")[:, 0:NE * HID].rearrange("p (e h) -> p e h", e=NE)
                dve.wait_ge(s_e1, 16)
                link(V.tensor_copy(ew1_hi[:], e1_in))
                dve.wait_ge(prep_dve, 4)
                tt(ew1_lo[:], e1_in, ew1_hi[:].bitcast(F32), ALU.subtract).then_inc(prep_dve, 1)
                dve.wait_ge(prep_pe, 3)
                dve.wait_ge(prep_dve, 5)
                V.tensor_copy(bias_cols[:], wide[1][:, 0:NL1 + 1]).then_inc(prep_dve, 1)

            def row_stats(b, n, jobs):
                if later(b, 1):
                    dve.wait_ge(s_x, 16 * TT)
                else:
                    dve.wait_ge(s_x0, 16)
                for t in range(TT):
                    ins = V.bn_stats(stats[:, t, :], x_all[:, b, t, :])
                link(ins)
                even, odd = stats[:, :, 0:3], stats[:, :, 3:6]
                tt(mv[:, 0, :], even[:, :, 1], odd[:, :, 1], ALU.add)
                tt(mv[:, 1, :], even[:, :, 1], odd[:, :, 1], ALU.subtract)
                link(tt(mv[:, 2, :], even[:, :, 2], odd[:, :, 2], ALU.add))
                ts(mean[:], mv[:, 0, :], 0.5, None, ALU.mult)
                ts(mv[:, 3, :], mv[:, 2, :], 1.0 / E, EPS, ALU.mult, ALU.add)
                link(tt(mv[:, 4, :], mv[:, 1, :], mv[:, 1, :], ALU.mult))
                stt(out=var_eps[:], in0=mv[:, 4, :], scalar=0.25, in1=mv[:, 3, :], op0=ALU.mult,
                    op1=ALU.add).then_inc(var_ready, 1)

            def norm(b, n, jobs):
                dve.wait_ge(rstd_ready, b + 1)
                for t in range(TT):
                    ins = ts(xn[:, t, :], x_all[:, b, t, :], mean[:, t:t + 1], rstd[:, t:t + 1],
                             ALU.subtract, ALU.mult)
                ins.then_inc(xn_ready, 1)
                if not later(b, 1):
                    dve.wait_ge(dve_step, 1)
                    constant_rows()
                    attention_weights()

            def x_cols(b, n, jobs):
                ps = wait_full(dve, jobs, ("x_cols", n))
                dve.wait_ge(x_hi_ready, 2 * b + 2)
                tt(x_lo[:], ps[:], x_hi[:].bitcast(F32), ALU.subtract).then_inc(x_lo_ready, 1)

            def proj(b, n, jobs):
                ps = wait_full(dve, jobs, ("proj", n))
                if isinstance(b, int) and b == 0 and n == 0:
                    dve.wait_ge(s_table, 32)
                which, term = divmod(n, 2)
                tt(rope_t[:, which, term, :], ps[:], (cos_sb, sin_sb)[term][:], ALU.mult).then_inc(rope_ready, 1)

            def split(b, which, jobs):
                dve.wait_ge(rope_ready, 4 * b + 2 * which + 2)
                tt(roped[:, which, :], rope_t[:, which, 0, :], rope_t[:, which, 1, :],
                   ALU.add).then_inc(roped_ready, 1)
                if which == 0 and later(b, 1):
                    for g in range(NG):
                        dve.wait_ge(q_in[g], 48 * b)
                        dve.wait_ge(k_in[g], 48 * b)
                dve.wait_ge(roped_ready, 2 * b + which + 1)
                V.tensor_copy(roped_hi[:, which, :], roped[:, which, :]).then_inc(hi_ready, 1)
                dve.wait_ge(hi_ready, 2 * b + which + 1)
                tt(roped_lo[:, which, :], roped[:, which, :], roped_hi[:, which, :].bitcast(F32),
                   ALU.subtract).then_inc(lo_ready, 1)

            def wide4(ap):
                return ap.unsqueeze(2).to_broadcast([P, TT, NE])

            def logits(b, n, jobs):
                ps = wait_full(dve, jobs, ("logits", n))
                tt(lg[:, 0], ps[:, 0:TT * NE].rearrange("p (t e) -> p t e", e=NE),
                   rb2_bc[:].unsqueeze(1).to_broadcast([P, TT, NE]), ALU.add).then_inc(logits_read, 1)
                dve.wait_ge(logits_read, b + 1)

            def top_two(b, n, jobs):
                if n > 0:
                    dve.wait_ge(dve_step, steps[1] + steps[0])
                k, m = divmod(n, 6)
                a, eq, key, one = (lg[:, 5 * k + i] for i in range(4))
                if m == 0:
                    ins = V.tensor_reduce(top[:, k, :], a, AX, ALU.max)
                elif m == 1:
                    ins = tt(eq, a, wide4(top[:, k, :]), ALU.is_equal)
                elif m == 2:
                    ins = tt(key, eq, rank[:].unsqueeze(1).to_broadcast([P, TT, NE]), ALU.mult)
                elif m == 3:
                    ins = V.tensor_reduce(top[:, 2 + k, :], key, AX, ALU.max)
                elif m == 4:
                    ins = tt(one, key, wide4(top[:, 2 + k, :]), ALU.is_equal)
                else:
                    ins = stt(out=lg[:, 5], in0=one, scalar=-3.0e38, in1=a, op0=ALU.mult, op1=ALU.add)
                ins.then_inc(dve_step, 1)
                steps[0] += 1
                if n == NTOP - 1:
                    tt(top[:, 4, :], top[:, 1, :], top[:, 0, :], ALU.subtract).then_inc(gap_ready, 1)

            def weights(b, n, jobs):
                dve.wait_ge(tanh_ready, b + 1)
                ts(top[:, 6, :], top[:, 5, :], -0.5, 0.5, ALU.mult, ALU.add)
                link(ts(top[:, 7, :], top[:, 5, :], 0.5, 0.5, ALU.mult, ALU.add))
                tt(lg[:, 4], lg[:, 3], top[:, 6, :].unsqueeze(2).to_broadcast([P, TT, NE]), ALU.mult)
                link(tt(lg[:, 9], lg[:, 8], top[:, 7, :].unsqueeze(2).to_broadcast([P, TT, NE]), ALU.mult))
                tt(gate_w[:], lg[:, 4], lg[:, 9], ALU.add).then_inc(w_ready, 1)

            def max0(b, n, jobs):
                i, r = divmod(n, GH)
                ps = wait_full(dve, jobs, ("max0", n))
                V.tensor_reduce(row_max[:, 0, i, r:r + 1], ps[:, 0:(i + 1) * P], AX, ALU.max).then_inc(max0_done, 1)

            def max_scores(b, m, jobs):
                g, i, pair = 1 + m // NPAIR, m % NPAIR // 2, m % 2
                dve.wait_ge(max_full, NMAX * b + m + 1)
                V.tensor_reduce(row_max[:, g, i, 2 * pair:2 * pair + 2],
                                ring[:, 2 * (m % 2):2 * (m % 2) + 2, 0:(i + 1) * P], AX, ALU.max).then_inc(max_done, 1)

            def negate(b, g, jobs):
                if g == 0:
                    dve.wait_ge(max0_done, NMAX0 * b + NMAX0)
                else:
                    dve.wait_ge(max_done, NMAX * b + NPAIR * g)
                link(ts(neg_max[:, g, :, 0:GH].bitcast(F32R), row_max[:, g], -1.0, None, ALU.mult))
                stt(out=neg_max[:, g, :, GH:2 * GH].bitcast(F32R), in0=row_max[:, g], scalar=-1.0,
                    in1=neg_max[:, g, :, 0:GH], op0=ALU.mult, op1=ALU.subtract).then_inc(neg_ready, 1)

            def router(b, n, jobs):
                if not later(b, 1):
                    ffn_weights()

            def heads(b, g, jobs):
                if isinstance(b, int) and b == 0 and g == 0:
                    dve.wait_ge(s_const, 16 * (2 + NG))
                dve.wait_ge(k_in[g], 48 * b + 48)
                for r in range(GH):
                    last = ts(k_head[:, GH * g + r, :], k_stack[:, g, :], hmask[:, r:r + 1], None, ALU.mult)
                last.then_inc(heads_ready, 1)

            def pv(b, n, jobs):
                g, j = divmod(n, 3)
                if j == 2:
                    dve.wait_ge(pv_done, NSTEP * b + n + 1)
                    V.tensor_copy(o_cols[:, g, :], wide[g % 2][:]).then_inc(o_done, 1)

            def values(b, n, jobs):
                ps = wait_full(dve, jobs, ("values", n))
                if later(b, 1):
                    dve.wait_ge(pv_done, NSTEP * b)
                V.tensor_copy(v_cols[:, :, :, 0:D],
                              ps[:].rearrange("p (t h d) -> p t h d", t=TT, h=H)).then_inc(v_ready, 1)

            def layer2(b, e, jobs):
                ps = wait_full(dve, jobs, ("layer2", e))
                if e == 0:
                    dve.wait_ge(w_ready, b + 1)
                else:
                    dve.wait_ge(acc_ready, NE * b + e)
                for t in range(TT):
                    ins = stt(out=acc[:, t, :], in0=ps[:, t * E:(t + 1) * E], scalar=gate_w[:, t, e:e + 1],
                              in1=(xn if e == 0 else acc)[:, t, :], op0=ALU.mult, op1=ALU.add)
                ins.then_inc(acc_ready, 1)

            def expert_bias(b, n, jobs):
                ps = wait_full(dve, jobs, ("expert_bias", n))
                dve.wait_ge(acc_ready, NE * b + NE)
                tt(y_sum[:].rearrange("p t e -> p (t e)"), acc[:].rearrange("p t e -> p (t e)"), ps[:],
                   ALU.add).then_inc(y_ready, 1)

            def out_rows(b, i, jobs):
                ps = wait_full(dve, jobs, ("out_rows", i))
                cols = ps[:].rearrange("p (h c) -> p h c", h=H)
                link(V.reciprocal(inv_sum[:, i, :], cols[:, :, D]))
                tt(o_rows[:, i, :].rearrange("p (h d) -> p h d", h=H), cols[:, :, 0:D],
                   inv_sum[:, i, :].unsqueeze(2).to_broadcast([P, H, D]), ALU.mult).then_inc(rows_ready, 1)

            def project(b, n, jobs):
                ps = wait_full(dve, jobs, ("project", n))
                dve.wait_ge(g_ready, b + 1)
                if later(b, 1):
                    dve.wait_ge(out_ready, b)
                tt(gated[:].rearrange("p t e -> p (t e)"), ps[:], g_silu[:].rearrange("p t e -> p (t e)"),
                   ALU.mult).then_inc(gated_ready, 1)

            do = {"router": router, "stats": row_stats, "norm": norm, "x_cols": x_cols, "proj": proj, "split": split,
                  "logits": logits,
                  "top": top_two, "weights": weights, "max0": max0, "max": max_scores, "negate": negate, "heads": heads, "pv": pv,
                  "values": values, "layer2": layer2, "expert_bias": expert_bias,
                  "out_rows": out_rows, "project": project}

            prologue(do)
            first_round(do)
            before = steps[0] + steps[1]
            steps[0] = 0
            with dve.Fori(1, B - 1) as b:
                steps[1] = before + (b - 1) * PER_LINKS
                middle_round(do, b)
                assert steps[0] == PER_LINKS, steps
            steps[:] = 0, before + (B - 2) * PER_LINKS
            last_round(do)

        @block.gpsimd
        def _(pool):
            G = nc.gpsimd

            def row_stats(b, n, jobs):
                pool.wait_ge(var_ready, b + 1)
                if isinstance(b, int) and b == 0:
                    pool.wait_ge(prep_dve, 1)
                if later(b, 1):
                    pool.wait_ge(xn_ready, b)
                G.tensor_tensor(rstd[:], var_eps[:], half_exp[:], ALU.pow).then_inc(rstd_ready, 1)

            def project(b, n, jobs):
                pool.wait_ge(gated_ready, b + 1)
                if later(b, 1):
                    pool.wait_ge(stored, 16 * b)
                G.tensor_tensor(out_sb[:], gated[:], x_all[:, b, :, :], ALU.add).then_inc(out_ready, 1)

            run(pool, {"stats": row_stats, "project": project})


PER_LINKS = sum({"top": 1, "weights": 2, "out_rows": 1, "stats": 3, "negate": 1}.get(s[0], 0)
                for s in STAGE_B + STAGE_C)


_INS = ["L0_attn_x", "L0_attn_wq", "L0_attn_w_down", "L0_attn_wk_up", "L0_attn_wv_up", "L0_attn_wo",
        "L0_ffn_rw1", "L0_ffn_rb1", "L0_ffn_rw2", "L0_ffn_rb2", "L0_ffn_ew1", "L0_ffn_eb1", "L0_ffn_ew2",
        "L0_ffn_eb2"]


def shape_constants():
    inv = 1.0 / 10000.0 ** (np.arange(0, D, 2, dtype=np.float32) / D)
    ang = np.outer(np.arange(T, dtype=np.float32), inv)
    spread = lambda a: np.ascontiguousarray(np.tile(np.repeat(a.T.astype(np.float32), 2, axis=0), (H, 1)))
    t = np.arange(T)
    tile, page = t // P, t % P // PAGE
    key_rows = np.zeros((P - MASK0, T), np.float32)
    query_rows = np.zeros((P - MASK0, T), np.float32)
    for j in range(TT):
        for a in range(3):
            key_rows[3 * j + a] = (tile == j) & (page > a)
            query_rows[3 * j + a] = np.where((tile == j) & (page == a), -BIG, 0.0)
    key_rows[MAX0 - MASK0:MAX0 - MASK0 + MAX_SLOT] = 1.0
    row = np.arange(P)
    head_mask = np.zeros((P, GH), np.float32)
    for r in range(GH):
        head_mask[:, r] = ((row < MASK0) & (row % 32 // D == r)) | ((row >= MASK0) & (row < MAX0)) | (
            (row >= MAX0) & (row < MAX0 + MAX_SLOT) & ((row - MAX0) % GH == r))
    return {"cos_t": spread(np.cos(ang)), "sin_t": spread(np.sin(ang)), "ident_c": np.eye(P, dtype=np.float32),
            "key_rows": key_rows, "query_rows": query_rows, "head_mask": head_mask,
            "rank_c": np.arange(NE, 0, -1).astype(np.float32)}


def kernel(**inputs):
    import concourse.bacc as bacc
    from concourse.bass_utils import run_bass_kernel_spmd

    nc = bacc.Bacc("TRN2", target_bir_lowering=False, num_devices=1)
    arrays, args = {}, []
    for name, a in [(n, np.ascontiguousarray(inputs[n])) for n in _INS] + list(shape_constants().items()):
        arrays[f"in_{name}"] = a
        args.append(nc.dram_tensor(f"in_{name}", a.shape, mybir.dt.from_np(a.dtype), kind="ExternalInput").ap())
    args.append(nc.dram_tensor("out_0", (B, T, E), F32, kind="ExternalOutput").ap())
    build(nc, *args)
    return run_bass_kernel_spmd(nc, [arrays], core_ids=[0]).results[0]["out_0"]
```
